# Optimizing a Trainium2 kernel written in Bass

```python
import numpy as np
import jax
import jax.numpy as jnp

def _softmax(x, axis=-1):
    return jax.nn.softmax(x, axis=axis)

def _gelu(x):
    return jax.nn.gelu(x, approximate=True)

def _silu(x):
    return jax.nn.silu(x)

def _sigmoid(x):
    return jax.nn.sigmoid(x)

def _layernorm(x, axis=-1, eps=1e-05):
    m = jnp.mean(x, axis=axis, keepdims=True)
    v = jnp.var(x, axis=axis, keepdims=True)
    return (x - m) / jnp.sqrt(v + eps)

def _scatter_add(tgt, idx, src, axis=0):
    return tgt.at[idx].add(src)

def _segment_sum(src, seg, n):
    return jax.ops.segment_sum(src, seg, n)
kernel_name = 'mk_dlrm_tower_d1_rec_r8_65f806'

def setup_inputs(seed: int=0):
    np.random.seed(seed)
    _w = jnp.asarray

    def _rec_inputs():
        import jax
        import jax.numpy as jnp
        _tk = jax.random.key(seed)
        dense_ctx = jax.random.normal(jax.random.fold_in(_tk, 190), (512, 16), jnp.float32)
        ids = jnp.stack([jax.random.randint(jax.random.fold_in(_tk, 200 + f), (512,), 0, v, jnp.int32) for f, v in enumerate([12500, 1250, 1000, 12500, 1000, 1250, 1250, 1250])], axis=1)
        tbl_0 = 0.05 * jax.random.normal(jax.random.fold_in(_tk, 500 + 0), (12500, 1024), jnp.float32)
        tbl_1 = 0.05 * jax.random.normal(jax.random.fold_in(_tk, 500 + 1), (1250, 1024), jnp.float32)
        tbl_2 = 0.05 * jax.random.normal(jax.random.fold_in(_tk, 500 + 2), (1000, 1024), jnp.float32)
        tbl_3 = 0.05 * jax.random.normal(jax.random.fold_in(_tk, 500 + 3), (12500, 1024), jnp.float32)
        tbl_4 = 0.05 * jax.random.normal(jax.random.fold_in(_tk, 500 + 4), (1000, 1024), jnp.float32)
        tbl_5 = 0.05 * jax.random.normal(jax.random.fold_in(_tk, 500 + 5), (1250, 1024), jnp.float32)
        tbl_6 = 0.05 * jax.random.normal(jax.random.fold_in(_tk, 500 + 6), (1250, 1024), jnp.float32)
        tbl_7 = 0.05 * jax.random.normal(jax.random.fold_in(_tk, 500 + 7), (1250, 1024), jnp.float32)
        _rk = jax.random.fold_in(_tk, 7)
        W_top1 = 0.0310087 * jax.random.normal(jax.random.fold_in(_tk, 801), (1040, 512), jnp.float32)
        W_top2 = 0.0441942 * jax.random.normal(jax.random.fold_in(_tk, 802), (512, 256), jnp.float32)
        W_top3 = 0.0625 * jax.random.normal(jax.random.fold_in(_tk, 803), (256, 1), jnp.float32)
        b_top1 = jnp.zeros((512,), jnp.float32)
        b_top2 = jnp.zeros((256,), jnp.float32)
        return (dense_ctx, ids, tbl_0, tbl_1, tbl_2, tbl_3, tbl_4, tbl_5, tbl_6, tbl_7, W_top1, b_top1, W_top2, b_top2, W_top3)
    dense_ctx, ids, tbl_0, tbl_1, tbl_2, tbl_3, tbl_4, tbl_5, tbl_6, tbl_7, W_top1, b_top1, W_top2, b_top2, W_top3 = _rec_inputs()

    def _L0_rec_setup():
        import jax, jax.numpy as jnp
        import numpy as np
        B, F, H = (1024, 8, 1024)

        def _linear_params(key, fan_in, fan_out):
            kw, kb = jax.random.split(key)
            w = jax.random.normal(kw, (fan_in, fan_out), dtype=jnp.float32) * 0.02
            b = jax.random.normal(kb, (fan_out,), dtype=jnp.float32) * 0.02
            return (w, b)
        key = jax.random.key(seed)
        ks = jax.random.split(key, 7)
        field_vectors = jax.random.normal(ks[0], (B, F, H), dtype=jnp.float32)
        Wn1, bn1 = _linear_params(ks[1], H, H)
        Wn2, bn2 = _linear_params(ks[2], H, H)
        Wa1, ba1 = _linear_params(ks[3], 2 * H, H)
        Wa2, ba2 = _linear_params(ks[4], H, H)
        Wo1, bo1 = _linear_params(ks[5], 2 * H, H)
        Wo2, bo2 = _linear_params(ks[6], H, H)
        not_idx = jnp.array([2, 3], dtype=jnp.int64)
        and_pairs = jnp.array([[0, 1], [2, 3]], dtype=jnp.int64)
        or_pairs = jnp.array([[4, 5]], dtype=jnp.int64)
        return {'field_vectors': field_vectors, 'Wn1': Wn1, 'bn1': bn1, 'Wn2': Wn2, 'bn2': bn2, 'Wa1': Wa1, 'ba1': ba1, 'Wa2': Wa2, 'ba2': ba2, 'Wo1': Wo1, 'bo1': bo1, 'Wo2': Wo2, 'bo2': bo2, 'not_idx': not_idx, 'and_pairs': and_pairs, 'or_pairs': or_pairs}
    _L0_rec_all = _L0_rec_setup()
    _L0_rec_in = {k: v for k, v in _L0_rec_all.items() if k in ('Wn1', 'bn1', 'Wn2', 'bn2', 'Wa1', 'ba1', 'Wa2', 'ba2', 'Wo1', 'bo1', 'Wo2', 'bo2', 'not_idx', 'and_pairs', 'or_pairs')}
    del _L0_rec_all
    return {'dense_ctx': dense_ctx, 'ids': ids, 'tbl_0': tbl_0, 'tbl_1': tbl_1, 'tbl_2': tbl_2, 'tbl_3': tbl_3, 'tbl_4': tbl_4, 'tbl_5': tbl_5, 'tbl_6': tbl_6, 'tbl_7': tbl_7, 'W_top1': W_top1, 'b_top1': b_top1, 'W_top2': W_top2, 'b_top2': b_top2, 'W_top3': W_top3, 'L0_rec_Wn1': _L0_rec_in['Wn1'], 'L0_rec_bn1': _L0_rec_in['bn1'], 'L0_rec_Wn2': _L0_rec_in['Wn2'], 'L0_rec_bn2': _L0_rec_in['bn2'], 'L0_rec_Wa1': _L0_rec_in['Wa1'], 'L0_rec_ba1': _L0_rec_in['ba1'], 'L0_rec_Wa2': _L0_rec_in['Wa2'], 'L0_rec_ba2': _L0_rec_in['ba2'], 'L0_rec_Wo1': _L0_rec_in['Wo1'], 'L0_rec_bo1': _L0_rec_in['bo1'], 'L0_rec_Wo2': _L0_rec_in['Wo2'], 'L0_rec_bo2': _L0_rec_in['bo2'], 'L0_rec_not_idx': _L0_rec_in['not_idx'], 'L0_rec_and_pairs': _L0_rec_in['and_pairs'], 'L0_rec_or_pairs': _L0_rec_in['or_pairs']}

def reference(dense_ctx, ids, tbl_0, tbl_1, tbl_2, tbl_3, tbl_4, tbl_5, tbl_6, tbl_7, W_top1, b_top1, W_top2, b_top2, W_top3, L0_rec_Wn1, L0_rec_bn1, L0_rec_Wn2, L0_rec_bn2, L0_rec_Wa1, L0_rec_ba1, L0_rec_Wa2, L0_rec_ba2, L0_rec_Wo1, L0_rec_bo1, L0_rec_Wo2, L0_rec_bo2, L0_rec_not_idx, L0_rec_and_pairs, L0_rec_or_pairs):
    import jax
    import jax.numpy as jnp

    def _L0_rec_ref(field_vectors, Wn1, bn1, Wn2, bn2, Wa1, ba1, Wa2, ba2, Wo1, bo1, Wo2, bo2, not_idx, and_pairs, or_pairs):
        import jax, jax.numpy as jnp
        import numpy as np
        B, F, H = (1024, 8, 1024)

        def _linear_params(key, fan_in, fan_out):
            kw, kb = jax.random.split(key)
            w = jax.random.normal(kw, (fan_in, fan_out), dtype=jnp.float32) * 0.02
            b = jax.random.normal(kb, (fan_out,), dtype=jnp.float32) * 0.02
            return (w, b)
        num_fields = field_vectors.shape[1]
        x_not = jnp.take(field_vectors, not_idx, axis=1)
        t = jnp.tanh(jax.nn.relu(x_not @ Wn1 + bn1) @ Wn2 + bn2)
        iv = field_vectors.at[:, not_idx, :].set(t)

        def pair_fuse(pairs, W1, b1, W2, b2):
            v = jnp.concatenate([jnp.take(iv, pairs[:, 0], axis=1), jnp.take(iv, pairs[:, 1], axis=1)], axis=-1)
            return jax.nn.relu(v @ W1 + b1) @ W2 + b2
        and_out = pair_fuse(and_pairs, Wa1, ba1, Wa2, ba2)
        or_out = pair_fuse(or_pairs, Wo1, bo1, Wo2, bo2)
        processed = jnp.zeros((num_fields,), dtype=field_vectors.dtype).at[and_pairs.reshape(-1)].set(1.0).at[or_pairs.reshape(-1)].set(1.0)
        remaining = 1.0 - processed
        sum_res = and_out.sum(axis=1) + or_out.sum(axis=1) + jnp.einsum('bfh,f->bh', iv, remaining)
        count = and_pairs.shape[0] + or_pairs.shape[0] + remaining.sum()
        return sum_res / count
    e = jnp.stack([tbl_0[ids[:, 0]], tbl_1[ids[:, 1]], tbl_2[ids[:, 2]], tbl_3[ids[:, 3]], tbl_4[ids[:, 4]], tbl_5[ids[:, 5]], tbl_6[ids[:, 6]], tbl_7[ids[:, 7]]], axis=1)
    z = _L0_rec_ref(e, L0_rec_Wn1, L0_rec_bn1, L0_rec_Wn2, L0_rec_bn2, L0_rec_Wa1, L0_rec_ba1, L0_rec_Wa2, L0_rec_ba2, L0_rec_Wo1, L0_rec_bo1, L0_rec_Wo2, L0_rec_bo2, L0_rec_not_idx, L0_rec_and_pairs, L0_rec_or_pairs)
    z = z.reshape(z.shape[0], -1)
    h = jnp.concatenate([z, dense_ctx], axis=1)
    h = jnp.maximum(h @ W_top1 + b_top1, 0.0)
    h = jnp.maximum(h @ W_top2 + b_top2, 0.0)
    y = h @ W_top3
    return y

_drawn_inputs = setup_inputs


def setup_inputs(seed=0):
    import zlib

    import numpy as np

    out = dict(_drawn_inputs(seed))
    spreads = {'b_top1': (0.0, 0.1), 'b_top2': (0.0, 0.1)}
    factors = {'tbl_0': 4.378,
     'tbl_1': 4.413,
     'tbl_2': 8.0,
     'tbl_3': 8.0,
     'tbl_4': 4.625,
     'tbl_5': 4.591,
     'L0_rec_Wn1': 8.0,
     'L0_rec_bn1': 8.0,
     'L0_rec_Wn2': 8.0,
     'L0_rec_bn2': 8.0,
     'L0_rec_Wa1': 2.959,
     'L0_rec_ba1': 3.822,
     'L0_rec_Wo1': 3.461,
     'L0_rec_bo1': 8.0,
     'L0_rec_Wo2': 2.905}
    for name, (base, spread) in spreads.items():
        noise = np.random.default_rng([zlib.crc32(name.encode()), seed]).standard_normal(out[name].shape)
        drawn = base * np.exp(spread * noise) if base else spread * noise
        out[name] = jnp.asarray(drawn.astype(out[name].dtype))
    for name, factor in factors.items():
        out[name] = (out[name] * factor).astype(out[name].dtype)
    return out
```

```python
from contextlib import ExitStack

import concourse.bass as bass
from concourse import mybir

P = 128
F32 = mybir.dt.float32
F32R = mybir.dt.float32r
I32 = mybir.dt.int32
ALU = mybir.AluOpType
ACT = mybir.ActivationFunctionType
AX = mybir.AxisListType

SCRATCH = 4096
N_NAT = 6
N_RAW = 4
N_SPLIT = 2
KG = 4
N_SLOTS = 8


def logic_tower(nc, dense, ids, fields, table, first_row, Wn1, Wn2, Wa1, Wa2, Wo1, Wo2, Wt1, Wt2, bias_rows, out):
    B, NF = ids.shape
    H = Wn1.shape[0]
    ND = dense.shape[1]
    T1, T2 = Wt1.shape[1], Wt2.shape[1]
    BT, KT = B // P, H // P
    M1, M2 = T1 // P, T2 // P
    N_BIAS = bias_rows.shape[0]
    assert B == 512 and KT == 2 * KG and M1 == KG and NF == 8 and ND <= P

    S_NOT1, S_NOT2, S_AND1, S_OR1, S_MIX, S_TOP1 = (n * KT for n in range(6))
    S_TOP2 = S_TOP1 + M1
    S_Y = S_TOP2 + M2
    G_NOT1, G_NOT2, G_AND1 = 0, 2 * KT, 4 * KT
    G_OR1, G_MIX, G_TOP1 = G_AND1 + 4 * KT, G_AND1 + 8 * KT, G_AND1 + 12 * KT
    G_TOP2 = G_TOP1 + 2 * M1
    C_N1, C_N2, C_A1, C_A2, C_O1, C_O2, C_T1 = (n * KT for n in range(7))
    C_T2 = C_T1 + M1
    C_W3 = C_T2 + M2
    assert N_BIAS == C_W3 + M2
    U_REM = N_SLOTS * BT

    with ExitStack() as ctx:
        def sb(name, shape, dt):
            return ctx.enter_context(nc.sbuf_tensor(name, shape, dt))

        def sem(name):
            return ctx.enter_context(nc.semaphore(name))

        x_hi = sb("x_hi", [P, 4, KT, B], F32R)
        x_lo = sb("x_lo", [P, 4, KT, B], F32R)
        tanh_out = sb("tanh_out", [P, 2, KT, B], F32)
        and_hidden = sb("and_hidden", [P, KT, B], F32)
        nat = sb("nat", [P, N_NAT, H], F32)
        w_raw = sb("w_raw", [P, N_RAW, KG, P], F32)
        w_hi = sb("w_hi", [P, N_SPLIT, KG, P], F32R)
        w_lo = sb("w_lo", [P, N_SPLIT, KG, P], F32R)
        ident = sb("ident", [P, P], F32)
        bias = sb("bias", [P, N_BIAS], F32)
        mix_bias = sb("mix_bias", [P, KT], F32)
        rows_i = sb("rows_i", [P, BT, N_SLOTS], I32)
        field_rows_i = sb("field_rows_i", [P, BT, NF], I32)
        rem_e = sb("rem_e", [P, NF], F32)
        rem_t = sb("rem_t", [P, 2], F32)
        one_by_count = sb("one_by_count", [P, 1], F32)
        flags = sb("flags", [P, 2, N_SLOTS], I32)
        rem_rows = tanh_out[:, 0, :, :].rearrange("p k b -> p (k b)").rearrange("p (t h) -> p t h", t=BT)
        rem_sum = tanh_out[:, 1, :, :].rearrange("p k b -> p (k b)").rearrange("p (t h) -> p t h", t=BT)
        setup = and_hidden[:, :, :].rearrange("p k b -> p (k b)")
        used = [0]

        def scratch(n, dt=F32):
            at, used[0] = used[0], used[0] + n
            v = setup[:, at:at + n]
            return v if dt == F32 else v.bitcast(dt)

        ids_i = scratch(BT * NF, I32).rearrange("p (t f) -> p t f", t=BT)
        ids_f = scratch(BT * NF).rearrange("p (t f) -> p t f", t=BT)
        fields_i = scratch(N_SLOTS, I32)
        fields_f = scratch(N_SLOTS)
        first_i = scratch(NF, I32)
        first_f = scratch(NF)
        field_no_i = scratch(NF, I32)
        field_no = scratch(NF)
        is_field = scratch(N_SLOTS * NF).rearrange("p (s f) -> p s f", s=N_SLOTS)
        picked = scratch(BT * N_SLOTS * NF).rearrange("p (t s f) -> p t s f", t=BT, s=N_SLOTS)
        rows_f = scratch(BT * N_SLOTS).rearrange("p (t s) -> p t s", t=BT)
        is_not = scratch(3 * N_SLOTS).rearrange("p (a s) -> p a s", a=3)
        paired = scratch(NF)
        remains = scratch(NF)
        no_not = scratch(NF)
        pair_of = scratch(2 * N_SLOTS * NF).rearrange("p (a s f) -> p a s f", a=2, s=N_SLOTS)
        other = scratch(4)
        bias_raw = scratch(P)
        assert used[0] <= KT * B
        dense_nat = nat[:, 4, 0:BT * P].rearrange("p (t d) -> p t d", t=BT)
        dense_w = nat[:, 5, 0:T1]
        TAIL_W, TAIL_X = KT - 2, KT - 1
        top_out = tanh_out[:, 1, 0:M2, :]
        y_row = tanh_out[0:1, 1, M2, :]

        mm = ctx.enter_context(nc.psum_tensor("mm", [P, 2, 2, B], F32))
        tp = ctx.enter_context(nc.psum_tensor("tp", [P, 2, KT, P], F32))
        rem_dram = nc.dram_tensor("rem_dram", [P, BT, H], F32, kind="Internal").ap()

        ids_in = sem("ids_in")
        fields_in = sem("fields_in")
        first_in = sem("first_in")
        bias_in = sem("bias_in")
        dense_in = sem("dense_in")
        dense_w_in = sem("dense_w_in")
        nat_in = [sem(f"nat_in{n}") for n in range(N_NAT)]
        rem_in = [sem(f"rem_in{n}") for n in range(BT)]
        raw_in = [sem(f"raw_in{n}") for n in range(N_RAW)]
        const_made = sem("const_made")
        setup_step = sem("setup_step")
        rows_ready = sem("rows_ready")
        flags_ready = sem("flags_ready")
        bias_turned = sem("bias_turned")
        bias_ready = sem("bias_ready")
        rem_used = sem("rem_used")
        rem_stored = sem("rem_stored")
        rem_back = sem("rem_back")
        tail_zeroed = sem("tail_zeroed")
        tail_turned = sem("tail_turned")
        tail_hi = sem("tail_hi")
        tail_ready = sem("tail_ready")
        w_hi_ready = sem("w_hi_ready")
        w_ready = sem("w_ready")
        w_used = sem("w_used")
        transposed = sem("transposed")
        fill_hi = sem("fill_hi")
        filled = sem("filled")
        act_step = sem("act_step")
        evac_act = sem("evac_act")
        and_hi = sem("and_hi")
        and_ready = sem("and_ready")
        mix_step = sem("mix_step")
        mix_sum = sem("mix_sum")
        evacuated = sem("evacuated")
        y_done = sem("y_done")
        y_ready = sem("y_ready")
        stored = sem("stored")

        block = ctx.enter_context(nc.Block())

        @block.sync
        def _(sp):
            def granule(w, k_tile, m, g, q):
                if not (isinstance(g, int) and g < N_RAW):
                    sp.wait_ge(w_ready, g - N_RAW + 1)
                src = w[k_tile * P:(k_tile + KG) * P, bass.ds(m * P, P)].rearrange("(k p) n -> p k n", p=P)
                sp.dma_start(w_raw[:, q, :, :], src).then_inc(raw_in[q], 16)

            def two_steps(parts, g0, i):
                for n in range(2 * len(parts)):
                    half, part = divmod(n, len(parts))
                    w, k_tile = parts[part]
                    granule(w, k_tile, i * 2 + half, i * (2 * len(parts)) + (g0 + n), (g0 + n) % N_RAW)

            not1 = [(Wn1, 0), (Wn1, KG)]
            two_steps(not1, G_NOT1, 0)
            with sp.Fori(1, KT // 2) as i:
                two_steps(not1, G_NOT1, i)
            with sp.Fori(0, KT // 2) as i:
                two_steps([(Wn2, 0), (Wn2, KG)], G_NOT2, i)
            with sp.Fori(0, KT // 2) as i:
                two_steps([(Wa1, n * KG) for n in range(4)], G_AND1, i)
            with sp.Fori(0, KT // 2) as i:
                two_steps([(Wo1, n * KG) for n in range(4)], G_OR1, i)
            with sp.Fori(0, KT // 2) as i:
                two_steps([(Wa2, 0), (Wa2, KG), (Wo2, 0), (Wo2, KG)], G_MIX, i)
            with sp.Fori(0, M1 // 2) as i:
                two_steps([(Wt1, 0), (Wt1, KG)], G_TOP1, i)
            for m in range(M2):
                granule(Wt2, 0, m, G_TOP2 + m, (G_TOP2 + m) % N_RAW)
            sp.wait_ge(y_ready, 1)
            sp.dma_start(out.rearrange("b o -> o b"), y_row).then_inc(stored, 16)
            sp.wait_ge(stored, 16)

        @block.gpsimd
        def _(pool):
            pool.iota(field_no_i, pattern=[[1, NF]], base=0, channel_multiplier=0).then_inc(const_made, 1)
            pool.memset(ident[:, :], 0.0).then_inc(const_made, 1)
            pool.memset(rem_sum, 0.0).then_inc(const_made, 1)
            pool.wait_ge(const_made, 3)
            pool.affine_select(out=ident[:, :], in_=ident[:, :], compare_op=ALU.not_equal, fill=1.0, base=0,
                               pattern=[[-1, P]], channel_multiplier=1).then_inc(const_made, 1)

            def gather(u):
                slot, bt = divmod(u, BT)
                if u >= N_NAT:
                    pool.wait_ge(transposed, u - N_NAT + 1)
                pool.indirect_dma_start(
                    nat[:, u % N_NAT, :], None, table,
                    bass.IndirectOffsetOnAxis(ap=rows_i[:, bt, slot:slot + 1], axis=0)
                ).then_inc(nat_in[u % N_NAT], 16)

            pool.wait_ge(rows_ready, 1)
            for u in range(2 * BT):
                gather(u)
            pool.wait_ge(rows_ready, 2)
            for f in range(NF):
                for bt in range(BT):
                    if f:
                        pool.wait_ge(rem_used, (f - 1) * BT + bt + 1)
                    pool.indirect_dma_start(
                        rem_rows[:, bt, :], None, table,
                        bass.IndirectOffsetOnAxis(ap=field_rows_i[:, bt, f:f + 1], axis=0)
                    ).then_inc(rem_in[bt], 16)
            pool.wait_ge(rem_used, NF * BT)
            pool.dma_start(rem_dram, rem_sum).then_inc(rem_stored, 16)
            for u in range(2 * BT, U_REM):
                gather(u)
            pool.wait_ge(transposed, U_REM)
            pool.wait_ge(rem_stored, 16)
            pool.dma_start(nat[:, 0:BT, :], rem_dram).then_inc(rem_back, 16)
            pool.memset(nat[:, BT:BT + 2, 0:B], 0.0).then_inc(tail_zeroed, 1)
            pool.wait_ge(tail_zeroed, 1)
            pool.dma_start(dense_nat[:, :, 0:ND], dense.rearrange("(t p) d -> p t d", p=P)).then_inc(dense_in, 16)
            pool.dma_start(dense_w[0:ND, :], Wt1[H:H + ND, :]).then_inc(dense_w_in, 16)

        @block.tensor
        def _(pe):
            def transpose_rows(u):
                if u < U_REM:
                    pe.wait_ge(nat_in[u % N_NAT], 16 * (u // N_NAT + 1))
                    buf = u % N_NAT
                else:
                    pe.wait_ge(rem_back, 16)
                    buf = u - U_REM
                if u >= 2:
                    pe.wait_ge(filled, u - 1)
                for k in range(KT):
                    last = pe.transpose(tp[:, u % 2, k, :], nat[:, buf, k * P:(k + 1) * P], ident[:, :])
                last.then_inc(transposed, 1)

            def products(bank, wh, wl, x, k, first, last):
                for j, buf in enumerate(x):
                    pe.matmul(bank[:, j, :], wh, x_hi[:, buf, k, :], start=first, stop=False)
                    pe.matmul(bank[:, j, :], wh, x_lo[:, buf, k, :], start=False, stop=False)
                for j, buf in enumerate(x):
                    ins = pe.matmul(bank[:, j, :], wl, x_hi[:, buf, k, :], start=False, stop=last)
                return ins

            def step(t, g, parity, operands, before=None, after=None, q0=0, dense_m=None):
                bank = mm[:, parity, :, :]
                pe.wait_ge(evacuated, t - 1) if not (isinstance(t, int) and t < 2) else None
                if dense_m is not None:
                    pe.wait_ge(tail_ready, 2)
                    cols = slice(dense_m * P, (dense_m + 1) * P)
                    products(bank, x_hi[:, 1, TAIL_W, cols], x_lo[:, 1, TAIL_W, cols], (1,), TAIL_X, True, False)
                n = sum(size for _, size in operands)
                tiles = [(x, k) for x, size in operands for k in range(size)]
                for at, (x, k) in enumerate(tiles):
                    if at % KG == 0:
                        pe.wait_ge(w_ready, g + at // KG + 1)
                    if before and at in before:
                        pe.wait_ge(*before[at])
                    q = (q0 + at // KG) % N_SPLIT
                    ins = products(bank, w_hi[:, q, at % KG, :], w_lo[:, q, at % KG, :], x, k,
                                   at == 0 and dense_m is None, at == n - 1)
                    if at % KG == KG - 1:
                        ins.then_inc(w_used, 1)
                    if after and at in after:
                        transpose_rows(after[at])

            def stage(t0, g0, operands, first, last, before):
                granules = sum(size for _, size in operands) // KG
                with pe.Fori(first, last) as i:
                    for half in range(2):
                        step(i * 2 + (t0 + half), i * (2 * granules) + (g0 + half * granules), half, operands, before)

            pe.wait_ge(bias_in, 16)
            pe.wait_ge(const_made, 4)
            pe.transpose(mm[:, 0, 0, 0:N_BIAS], bias_raw[0:N_BIAS, :], ident[0:N_BIAS, 0:N_BIAS]).then_inc(bias_turned, 1)

            for u in range(2 * BT):
                transpose_rows(u)
            pe.wait_ge(bias_ready, 1)
            nots = [((0, 1), KT)]
            before = {0: (filled, 2 * BT)}
            for m in range(2):
                step(m, G_NOT1 + 2 * m, m, nots, before)
            stage(S_NOT1, G_NOT1, nots, 1, KT // 2, before)
            stage(S_NOT2, G_NOT2, [((2, 3), KT)], 0, KT // 2, {KT - 1: (evacuated, S_NOT2)})

            for u in range(2 * BT, 4 * BT):
                transpose_rows(u)
            pairs = [((0, 1), KT), ((2, 3), KT)]
            before = {0: (filled, 4 * BT), KT: (filled, 6 * BT)}
            step(S_AND1, G_AND1, 0, pairs, before, after={k: 4 * BT + k for k in range(KT)})
            step(S_AND1 + 1, G_AND1 + 4, 1, pairs, before)
            stage(S_AND1, G_AND1, pairs, 1, KT // 2 - 1, before)
            step(S_OR1 - 2, G_OR1 - 8, 0, pairs, before)
            step(S_OR1 - 1, G_OR1 - 4, 1, pairs, before, after={KT + k: 6 * BT + k for k in range(KT)})

            stage(S_OR1, G_OR1, [((0,), KT), ((1,), KT)], 0, KT // 2,
                  {0: (filled, 7 * BT), KT: (filled, 8 * BT)})

            mixed = [((2,), KT), ((3,), KT)]
            before = {KT - 1: (and_ready, KT), 2 * KT - 1: (evacuated, S_MIX)}
            step(S_MIX, G_MIX, 0, mixed, before, after={KT + 2 * n: U_REM + n for n in range(BT)})
            pe.wait_ge(dense_in, 16)
            pe.wait_ge(filled, U_REM + BT - 1)
            for bt in range(BT):
                last = pe.transpose(tp[:, 0, bt, :], dense_nat[:, bt, :], ident[:, :])
            last.then_inc(tail_turned, 1)
            step(S_MIX + 1, G_MIX + 4, 1, mixed, before)
            stage(S_MIX, G_MIX, mixed, 1, KT // 2, before)

            for m in range(M1):
                step(S_TOP1 + m, G_TOP1 + 2 * m, m % 2, [((0,), KT)], {KT - 1: (evacuated, S_TOP1)}, dense_m=m)
            for m in range(M2):
                step(S_TOP2 + m, G_TOP2 + m, m % 2, [((1,), KG)], {KG - 1: (evacuated, S_TOP2)}, q0=m)
            for m in range(M2):
                pe.wait_ge(evac_act, S_TOP2 + m + 1)
                last = pe.matmul(mm[0:1, 0, 0, :], bias[:, C_W3 + m:C_W3 + m + 1], top_out[:, m, :],
                                 start=m == 0, stop=m == M2 - 1)
            last.then_inc(y_done, 1)

        def column(c, m):
            return bias[:, bass.ds(m + c, 1)]

        def tile(t, m):
            return t[:, bass.ds(m, 1), :].rearrange("p k b -> p (k b)")

        @block.scalar
        def _(act):
            act.dma_start(ids_i, ids.rearrange("(t p) f -> p t f", p=P)).then_inc(ids_in, 16)
            act.dma_start(fields_i, fields.partition_broadcast(P)).then_inc(fields_in, 16)
            act.dma_start(first_i, first_row.partition_broadcast(P)).then_inc(first_in, 16)
            act.dma_start(bias_raw[0:N_BIAS, :], bias_rows).then_inc(bias_in, 16)

            def split(c, i=0, per=0):
                g = i * per + c
                act.wait_ge(raw_in[c % N_RAW], i * (16 * (per // N_RAW)) + 16 * (c // N_RAW + 1))
                if c >= N_SPLIT:
                    act.wait_ge(w_used, g - N_SPLIT + 1)
                act.activation(w_hi[:, c % N_SPLIT, :, :], w_raw[:, c % N_RAW, :, :], ACT.Copy).then_inc(w_hi_ready, 1)

            def fill(u, buf):
                slot, bt = divmod(u, BT)
                to = x_hi[:, buf, :, bt * P:(bt + 1) * P]
                act.wait_ge(transposed, u + 1)
                if slot < 2:
                    act.activation(to, tp[:, u % 2, :, :], ACT.Copy).then_inc(fill_hi, 1)
                    return
                with act.If(is_not_field[slot] == 0):
                    act.activation(to, tp[:, u % 2, :, :], ACT.Copy).then_inc(fill_hi, 1)
                with act.Else():
                    of = tanh_out[:, bass.ds(which_not[slot], 1), :, bt * P:(bt + 1) * P]
                    act.activation(to, of.rearrange("p a k b -> p (a k) b"), ACT.Copy).then_inc(fill_hi, 1)

            def to_hidden(bufs, c):
                def evac(m, t, parity):
                    n = len(bufs)
                    for j in range(n):
                        act.activation(mm[:, parity, j, :], mm[:, parity, j, :], ACT.Relu,
                                       bias=column(c, m)).then_inc(act_step, 1)
                    act.wait_ge(act_step, act_base[c] + m * n + n)
                    for j, buf in enumerate(bufs):
                        last = act.activation(tile(x_hi[:, buf, :, :], m), mm[:, parity, j, :], ACT.Copy)
                    last.then_inc(evac_act, 1)
                return evac

            act_base = {C_N1: 0, C_O1: 2 * KT, C_T1: 3 * KT}

            def not2_evac(m, t, parity):
                for j in range(2):
                    last = act.activation(mm[:, parity, j, :], mm[:, parity, j, :], ACT.Tanh, bias=column(C_N2, m))
                last.then_inc(evac_act, 1)

            def and_evac(m, t, parity):
                act.activation(tile(and_hidden, m), mm[:, parity, 0, :], ACT.Relu, bias=column(C_A1, m))
                act.activation(mm[:, parity, 1, :], mm[:, parity, 1, :], ACT.Relu,
                               bias=column(C_A1, m)).then_inc(evac_act, 1)

            def or_evac(m, t, parity):
                act.activation(tile(x_hi[:, 2, :, :], m), tile(and_hidden, m), ACT.Copy).then_inc(and_hi, 1)
                to_hidden((3,), C_O1)(m, t, parity)

            def mix_evac(m, t, parity):
                act.wait_ge(mix_sum, m + 1)
                act.activation(tile(x_hi[:, 0, :, :], m), tile(tanh_out[:, 0, :, :], m), ACT.Copy,
                               scale=one_by_count[:, 0:1]).then_inc(evac_act, 1)

            def step(i, half, t0, g0, granules, evac):
                per = 2 * granules
                c = g0 + half * granules
                for n in range(2, granules + 2):
                    split(c + n, i, per)
                act.wait_ge(w_used, i * per + c + granules)
                evac(i * 2 + half, i * 2 + (t0 + half), half)

            def stage(t0, g0, granules, evac, first=0, last=KT // 2):
                with act.Fori(first, last) as i:
                    for half in range(2):
                        step(i, half, t0, g0, granules, evac)

            split(0)
            split(1)
            for u in range(2 * BT):
                fill(u, u // BT)
            act.wait_ge(bias_ready, 1)
            stage(S_NOT1, G_NOT1, 2, to_hidden((2, 3), C_N1))
            stage(S_NOT2, G_NOT2, 2, not2_evac)

            act.wait_ge(flags_ready, 1)
            is_not_field = {s: act.value_load(flags[0:1, 0, s:s + 1], min_val=0, max_val=1) for s in range(2, N_SLOTS)}
            which_not = {s: act.value_load(flags[0:1, 1, s:s + 1], min_val=0, max_val=1) for s in range(2, N_SLOTS)}
            act.wait_ge(evacuated, S_AND1)
            for u in range(2 * BT, 6 * BT):
                fill(u, u // BT - 2)
            step(0, 0, S_AND1, G_AND1, 4, and_evac)
            step(0, 1, S_AND1, G_AND1, 4, and_evac)
            stage(S_AND1, G_AND1, 4, and_evac, 1, KT // 2 - 1)
            step(KT // 2 - 1, 0, S_AND1, G_AND1, 4, and_evac)
            split(G_OR1 - 2)
            split(G_OR1 - 1)
            act.wait_ge(w_used, G_OR1 - 2)
            for u in range(6 * BT, 7 * BT):
                fill(u, 0)
            split(G_OR1)
            for u in range(7 * BT, 8 * BT):
                fill(u, 1)
            split(G_OR1 + 1)
            act.wait_ge(w_used, G_OR1)
            and_evac(KT - 1, S_OR1 - 1, 1)
            stage(S_OR1, G_OR1, 4, or_evac)

            step(0, 0, S_MIX, G_MIX, 4, mix_evac)
            act.wait_ge(tail_turned, 1)
            act.activation(x_hi[:, 1, TAIL_X, :], tp[:, 0, 0:BT, :].rearrange("p t b -> p (t b)"),
                           ACT.Copy).then_inc(tail_hi, 1)
            act.wait_ge(dense_w_in, 16)
            act.activation(x_hi[:, 1, TAIL_W, :], dense_w, ACT.Copy).then_inc(tail_hi, 1)
            step(0, 1, S_MIX, G_MIX, 4, mix_evac)
            stage(S_MIX, G_MIX, 4, mix_evac, 1)

            for m in range(M1):
                c = G_TOP1 + 2 * m
                split(c + 2)
                split(c + 3)
                act.wait_ge(w_used, c + 2)
                to_hidden((1,), C_T1)(m, S_TOP1 + m, m % 2)
            for m in range(M2):
                act.wait_ge(w_used, G_TOP2 + m + 1)
                act.activation(top_out[:, m, :], mm[:, m, 0, :], ACT.Relu, bias=column(C_T2, m)).then_inc(evac_act, 1)
            act.wait_ge(y_done, 1)
            act.activation(y_row, mm[0:1, 0, 0, :], ACT.Copy).then_inc(y_ready, 1)

        @block.vector
        def _(dve):
            done = [0]

            def link(ins):
                done[0] += 1
                ins.then_inc(setup_step, 1)
                dve.wait_ge(setup_step, done[0])

            dve.wait_ge(fields_in, 16)
            dve.wait_ge(const_made, 3)
            dve.tensor_copy(fields_f, fields_i).then_inc(setup_step, 1)
            dve.tensor_copy(field_no, field_no_i).then_inc(setup_step, 1)
            dve.wait_ge(ids_in, 16)
            dve.wait_ge(first_in, 16)
            dve.tensor_copy(ids_f, ids_i).then_inc(setup_step, 1)
            done[0] = 3
            link(dve.tensor_copy(first_f, first_i))
            dve.tensor_tensor(ids_f, ids_f, first_f.unsqueeze(1).to_broadcast([P, BT, NF]), ALU.add).then_inc(setup_step, 1)
            done[0] = 5
            link(dve.tensor_tensor(is_field, fields_f.unsqueeze(2).to_broadcast([P, N_SLOTS, NF]),
                                   field_no.unsqueeze(1).to_broadcast([P, N_SLOTS, NF]), ALU.is_equal))
            for bt in range(BT):
                last = dve.tensor_tensor(picked[:, bt, :, :], is_field,
                                         ids_f[:, bt, :].unsqueeze(1).to_broadcast([P, N_SLOTS, NF]), ALU.mult)
            link(last)
            link(dve.tensor_reduce(rows_f, picked, AX.X, ALU.add))
            dve.tensor_copy(rows_i[:, :, :], rows_f).then_inc(rows_ready, 1)
            dve.tensor_copy(field_rows_i[:, :, :], ids_f).then_inc(rows_ready, 1)

            link(dve.tensor_reduce(paired, is_field[:, 2:N_SLOTS, :].rearrange("p s f -> p f s"), AX.X, ALU.max))
            link(dve.tensor_scalar(remains, paired, -1.0, 1.0, ALU.mult, ALU.add))
            link(dve.tensor_reduce(other[:, 0:1], remains, AX.X, ALU.add))
            link(dve.tensor_scalar(other[:, 0:1], other[:, 0:1], float((N_SLOTS - 2) // 2), None, ALU.add))
            dve.reciprocal(one_by_count[:, :], other[:, 0:1]).then_inc(setup_step, 1)
            done[0] += 1
            link(dve.tensor_tensor(no_not, is_field[:, 0, :], is_field[:, 1, :], ALU.max))
            link(dve.tensor_scalar(no_not, no_not, -1.0, 1.0, ALU.mult, ALU.add))
            link(dve.tensor_tensor(rem_e[:, :], remains, no_not, ALU.mult))
            for a in range(2):
                last = dve.tensor_tensor(pair_of[:, a, :, :], is_field,
                                         is_field[:, a, :].unsqueeze(1).to_broadcast([P, N_SLOTS, NF]), ALU.mult)
            link(last)
            link(dve.tensor_reduce(is_not[:, 0:2, :], pair_of, AX.X, ALU.add))
            dve.tensor_tensor(flags[:, 0, :], is_not[:, 0, :], is_not[:, 1, :], ALU.max).then_inc(setup_step, 1)
            done[0] += 1
            link(dve.tensor_scalar(flags[:, 1, :], is_not[:, 0, :], -1.0, 1.0, ALU.mult, ALU.add))
            link(dve.tensor_tensor(pair_of[:, 0, 0:2, :], is_field[:, 0:2, :],
                                   remains.unsqueeze(1).to_broadcast([P, 2, NF]), ALU.mult))
            link(dve.tensor_reduce(rem_t[:, :], pair_of[:, 0, 0:2, :], AX.X, ALU.add))
            link(dve.tensor_scalar(other[:, 1:2], is_not[:, 0, 1:2], -1.0, 1.0, ALU.mult, ALU.add))
            link(dve.tensor_tensor(rem_t[:, 1:2], rem_t[:, 1:2], other[:, 1:2], ALU.mult))
            dve.sem_inc(flags_ready, 1)

            dve.wait_ge(bias_turned, 1)
            link(dve.tensor_copy(bias[:, :], mm[:, 0, 0, 0:N_BIAS]))
            dve.scalar_tensor_tensor(mix_bias[:, :], bias[:, C_A2:C_A2 + KT], 2.0, bias[:, C_O2:C_O2 + KT],
                                     ALU.mult, ALU.add).then_inc(bias_ready, 1)

            def split(c, i=0, per=0):
                dve.wait_ge(w_hi_ready, i * per + c + 1)
                dve.tensor_tensor(w_lo[:, c % N_SPLIT, :, :], w_raw[:, c % N_RAW, :, :],
                                  w_hi[:, c % N_SPLIT, :, :].bitcast(F32), ALU.subtract).then_inc(w_ready, 1)

            def fill(u, buf):
                slot, bt = divmod(u, BT)
                cols = slice(bt * P, (bt + 1) * P)
                to, hi = x_lo[:, buf, :, cols], x_hi[:, buf, :, cols].bitcast(F32)
                dve.wait_ge(fill_hi, u + 1)
                if slot < 2:
                    dve.tensor_tensor(to, tp[:, u % 2, :, :], hi, ALU.subtract).then_inc(filled, 1)
                    return
                with dve.If(is_not_field[slot] == 0):
                    dve.tensor_tensor(to, tp[:, u % 2, :, :], hi, ALU.subtract).then_inc(filled, 1)
                with dve.Else():
                    of = tanh_out[:, bass.ds(which_not[slot], 1), :, cols].rearrange("p a k b -> p (a k) b")
                    dve.tensor_tensor(to, of, hi, ALU.subtract).then_inc(filled, 1)

            def lo_part(buf, m, src):
                return dve.tensor_tensor(tile(x_lo[:, buf, :, :], m), src,
                                         tile(x_hi[:, buf, :, :], m).bitcast(F32), ALU.subtract)

            def to_hidden(bufs):
                def evac(m, t, parity):
                    dve.wait_ge(evac_act, t + 1)
                    for j, buf in enumerate(bufs):
                        last = lo_part(buf, m, mm[:, parity, j, :])
                    last.then_inc(evacuated, 1)
                return evac

            def not2_evac(m, t, parity):
                dve.wait_ge(evac_act, t + 1)
                for j in range(2):
                    last = dve.tensor_copy(tile(tanh_out[:, j, :, :], m), mm[:, parity, j, :])
                last.then_inc(evacuated, 1)

            def and_evac(m, t, parity):
                dve.wait_ge(evac_act, t + 1)
                dve.tensor_tensor(tile(and_hidden, m), tile(and_hidden, m), mm[:, parity, 1, :],
                                  ALU.add).then_inc(evacuated, 1)

            def or_evac(m, t, parity):
                t0, t1 = tile(tanh_out[:, 0, :, :], m), tile(tanh_out[:, 1, :, :], m)
                dve.tensor_scalar(t0, t0, rem_t[:, 0:1], None, ALU.mult).then_inc(mix_step, 1)
                dve.wait_ge(and_hi, m + 1)
                lo_part(2, m, tile(and_hidden, m)).then_inc(and_ready, 1)
                dve.wait_ge(mix_step, m + 1)
                dve.scalar_tensor_tensor(t0, t1, rem_t[:, 1:2], t0, ALU.mult, ALU.add)
                to_hidden((3,))(m, t, parity)

            def mix_evac(m, t, parity):
                z = tile(tanh_out[:, 0, :, :], m)
                dve.wait_ge(w_used, mix_used(m))
                dve.scalar_tensor_tensor(z, mm[:, parity, 0, :], mix_bias[:, bass.ds(m, 1)], z, ALU.add,
                                         ALU.add).then_inc(mix_sum, 1)
                dve.wait_ge(evac_act, t + 1)
                dve.scalar_tensor_tensor(tile(x_lo[:, 0, :, :], m), z, one_by_count[:, 0:1],
                                         tile(x_hi[:, 0, :, :], m).bitcast(F32), ALU.mult,
                                         ALU.subtract).then_inc(evacuated, 1)

            def mix_used(m):
                return m * 4 + (G_MIX + 4)

            def step(i, half, t0, g0, granules, evac):
                per = 2 * granules
                c = g0 + half * granules
                for n in range(2, granules + 2):
                    split(c + n, i, per)
                evac(i * 2 + half, i * 2 + (t0 + half), half)

            def stage(t0, g0, granules, evac, first=0, last=KT // 2):
                with dve.Fori(first, last) as i:
                    for half in range(2):
                        step(i, half, t0, g0, granules, evac)

            def not1_evac(m, t, parity):
                to_hidden((2, 3))(m, t, parity)
                if not isinstance(m, int) or m:
                    dve.wait_ge(rem_used, m * BT)
                for bt in range(BT):
                    dve.wait_ge(rem_in[bt], m * 16 + 16)
                    dve.scalar_tensor_tensor(rem_sum[:, bt, :], rem_rows[:, bt, :], rem_e[:, bass.ds(m, 1)],
                                             rem_sum[:, bt, :], ALU.mult, ALU.add).then_inc(rem_used, 1)

            split(0)
            split(1)
            for u in range(2 * BT):
                fill(u, u // BT)
            step(0, 0, S_NOT1, G_NOT1, 2, not1_evac)
            step(0, 1, S_NOT1, G_NOT1, 2, not1_evac)
            stage(S_NOT1, G_NOT1, 2, not1_evac, 1)
            dve.wait_ge(rem_stored, 16)
            stage(S_NOT2, G_NOT2, 2, not2_evac)

            is_not_field = {s: dve.value_load(flags[0:1, 0, s:s + 1], min_val=0, max_val=1) for s in range(2, N_SLOTS)}
            which_not = {s: dve.value_load(flags[0:1, 1, s:s + 1], min_val=0, max_val=1) for s in range(2, N_SLOTS)}
            for u in range(2 * BT, 6 * BT):
                fill(u, u // BT - 2)
            step(0, 0, S_AND1, G_AND1, 4, and_evac)
            step(0, 1, S_AND1, G_AND1, 4, and_evac)
            stage(S_AND1, G_AND1, 4, and_evac, 1, KT // 2 - 1)
            step(KT // 2 - 1, 0, S_AND1, G_AND1, 4, and_evac)
            split(G_OR1 - 2)
            split(G_OR1 - 1)
            for u in range(6 * BT, 7 * BT):
                fill(u, 0)
            split(G_OR1)
            for u in range(7 * BT, 8 * BT):
                fill(u, 1)
            split(G_OR1 + 1)
            and_evac(KT - 1, S_OR1 - 1, 1)
            dve.wait_ge(evacuated, S_OR1)
            stage(S_OR1, G_OR1, 4, or_evac)

            split(G_MIX + 2)
            split(G_MIX + 3)
            dve.wait_ge(evacuated, S_MIX)
            for bt in range(BT):
                u = U_REM + bt
                part = tanh_out[:, 0, :, bt * P:(bt + 1) * P]
                dve.wait_ge(transposed, u + 1)
                dve.tensor_tensor(part, part, tp[:, u % 2, :, :], ALU.add).then_inc(filled, 1)
            split(G_MIX + 4)
            split(G_MIX + 5)
            dve.wait_ge(filled, U_REM + BT)
            mix_evac(0, S_MIX, 0)
            dve.wait_ge(tail_hi, 1)
            dve.tensor_tensor(x_lo[:, 1, TAIL_X, :], tp[:, 0, 0:BT, :].rearrange("p t b -> p (t b)"),
                              x_hi[:, 1, TAIL_X, :].bitcast(F32), ALU.subtract).then_inc(tail_ready, 1)
            dve.wait_ge(tail_hi, 2)
            dve.tensor_tensor(x_lo[:, 1, TAIL_W, :], dense_w, x_hi[:, 1, TAIL_W, :].bitcast(F32),
                              ALU.subtract).then_inc(tail_ready, 1)
            step(0, 1, S_MIX, G_MIX, 4, mix_evac)
            stage(S_MIX, G_MIX, 4, mix_evac, 1)
            for m in range(M1):
                c = G_TOP1 + 2 * m
                split(c + 2) if c + 2 < G_TOP2 + M2 else None
                split(c + 3) if c + 3 < G_TOP2 + M2 else None
                to_hidden((1,))(m, S_TOP1 + m, m % 2)


def kernel(dense_ctx, ids, tbl_0, tbl_1, tbl_2, tbl_3, tbl_4, tbl_5, tbl_6, tbl_7, W_top1, b_top1, W_top2, b_top2,
           W_top3, L0_rec_Wn1, L0_rec_bn1, L0_rec_Wn2, L0_rec_bn2, L0_rec_Wa1, L0_rec_ba1, L0_rec_Wa2, L0_rec_ba2,
           L0_rec_Wo1, L0_rec_bo1, L0_rec_Wo2, L0_rec_bo2, L0_rec_not_idx, L0_rec_and_pairs, L0_rec_or_pairs):
    import numpy as np
    import concourse.bacc as bacc
    from concourse.bass_utils import run_bass_kernel_spmd

    tables = [tbl_0, tbl_1, tbl_2, tbl_3, tbl_4, tbl_5, tbl_6, tbl_7]
    sizes = [t.shape[0] for t in tables]
    arrays = {
        "dense": dense_ctx,
        "ids": ids,
        "fields": np.concatenate([np.ravel(L0_rec_not_idx), np.ravel(np.transpose(L0_rec_and_pairs)),
                                  np.ravel(L0_rec_or_pairs)]),
        "table": np.concatenate(tables),
        "first_row": np.array([sum(sizes[:n]) for n in range(len(sizes))], np.int32),
        "Wn1": L0_rec_Wn1, "Wn2": L0_rec_Wn2, "Wa1": L0_rec_Wa1, "Wa2": L0_rec_Wa2,
        "Wo1": L0_rec_Wo1, "Wo2": L0_rec_Wo2, "Wt1": W_top1, "Wt2": W_top2,
        "bias_rows": np.concatenate([L0_rec_bn1, L0_rec_bn2, L0_rec_ba1, L0_rec_ba2, L0_rec_bo1, L0_rec_bo2,
                                     b_top1, b_top2, np.ravel(W_top3)]).reshape(-1, P),
    }
    arrays = {k: np.ascontiguousarray(v) for k, v in arrays.items()}
    nc = bacc.Bacc("TRN2", target_bir_lowering=False, num_devices=1, dynamic_dma_scratch_size=SCRATCH)
    aps = {k: nc.dram_tensor(k, v.shape, mybir.dt.from_np(v.dtype), kind="ExternalInput").ap()
           for k, v in arrays.items()}
    out = nc.dram_tensor("out", (ids.shape[0], 1), F32, kind="ExternalOutput").ap()
    logic_tower(nc, *aps.values(), out)
    return run_bass_kernel_spmd(nc, [arrays], core_ids=[0]).results[0]["out"]
```

```python
from contextlib import ExitStack

import concourse.bass as bass
from concourse import mybir

P = 128
F32 = mybir.dt.float32
F32R = mybir.dt.float32r
I32 = mybir.dt.int32
ALU = mybir.AluOpType
ACT = mybir.ActivationFunctionType
AX = mybir.AxisListType

SCRATCH = 4096
N_NAT = 6
N_RAW = 4
N_SPLIT = 2
KG = 4
N_SLOTS = 8


N_TURNED = 6
Q = 4
R = P // Q


def logic_tower(nc, dense, ids, fields, table, first_row, Wn1, Wn2, Wa1, Wa2, Wo1, Wo2, Wt1, Wt2, bias_rows, out):
    B, NF = ids.shape
    H = Wn1.shape[0]
    ND = dense.shape[1]
    T1, T2 = Wt1.shape[1], Wt2.shape[1]
    BT, KT = B // P, H // P
    M1, M2 = T1 // P, T2 // P
    N_BIAS = bias_rows.shape[0]
    assert B == 512 and KT == 2 * KG and M1 == KG and NF == 8 and ND <= P

    S_NOT1, S_NOT2, S_AND1, S_OR1, S_MIX, S_TOP1 = (n * KT for n in range(6))
    S_TOP2 = S_TOP1 + M1
    S_Y = S_TOP2 + M2
    G_NOT1, G_NOT2, G_AND1 = 0, 2 * KT, 4 * KT
    G_OR1, G_MIX, G_TOP1 = G_AND1 + 4 * KT, G_AND1 + 8 * KT, G_AND1 + 12 * KT
    G_TOP2 = G_TOP1 + 2 * M1
    C_N1, C_N2, C_A1, C_A2, C_O1, C_O2, C_T1 = (n * KT for n in range(7))
    C_T2 = C_T1 + M1
    C_W3 = C_T2 + M2
    assert N_BIAS == C_W3 + M2
    U_REM = N_SLOTS * BT
    U_PAIR = 2 * BT
    X_USES = [sum(u % N_NAT == n for u in range(U_PAIR)) for n in range(N_NAT)]

    with ExitStack() as ctx:
        def sb(name, shape, dt):
            return ctx.enter_context(nc.sbuf_tensor(name, shape, dt))

        def sem(name):
            return ctx.enter_context(nc.semaphore(name))

        x_hi = sb("x_hi", [P, 4, KT, B], F32R)
        x_lo = sb("x_lo", [P, 4, KT, B], F32R)
        tanh_out = sb("tanh_out", [P, 2, KT, B], F32)
        and_hidden = sb("and_hidden", [P, KT, B], F32)
        nat = sb("nat", [P, N_NAT, H], F32)
        w_raw = sb("w_raw", [P, N_RAW, KG, P], F32)
        w_hi = sb("w_hi", [P, N_SPLIT, KG, P], F32R)
        w_lo = sb("w_lo", [P, N_SPLIT, KG, P], F32R)
        ident = sb("ident", [P, P], F32)
        bias = sb("bias", [P, N_BIAS], F32)
        mix_bias = sb("mix_bias", [P, KT], F32)
        rows_i = sb("rows_i", [P, BT, 2], I32)
        quarter_rows = sb("quarter_rows", [P, BT * Q, N_SLOTS - 2], I32)
        field_rows_i = sb("field_rows_i", [P, BT, NF], I32)
        rem_e = sb("rem_e", [P, NF], F32)
        rem_t = sb("rem_t", [P, 2], F32)
        one_by_count = sb("one_by_count", [P, 1], F32)
        idle_act = sb("idle_act", [P, (U_REM - U_PAIR) // 3 + 2 * KT], F32)
        idle_dve = sb("idle_dve", [P, (U_REM - U_PAIR) // 3 + 2 * KT], F32)
        flags = sb("flags", [P, 2, N_SLOTS], I32)
        rem_rows = tanh_out[:, 0, :, :].rearrange("p k b -> p (k b)").rearrange("p (t h) -> p t h", t=BT)
        rem_sum = and_hidden[:, :, :].rearrange("p k b -> p (k b)").rearrange("p (t h) -> p t h", t=BT)
        setup = and_hidden[:, :, :].rearrange("p k b -> p (k b)")
        used = [0]

        def scratch(n, dt=F32):
            at, used[0] = used[0], used[0] + n
            v = setup[:, at:at + n]
            return v if dt == F32 else v.bitcast(dt)

        ids_i = scratch(BT * NF, I32).rearrange("p (t f) -> p t f", t=BT)
        ids_f = scratch(BT * NF).rearrange("p (t f) -> p t f", t=BT)
        fields_i = scratch(N_SLOTS, I32)
        fields_f = scratch(N_SLOTS)
        first_i = scratch(NF, I32)
        first_f = scratch(NF)
        field_no_i = scratch(NF, I32)
        field_no = scratch(NF)
        is_field = scratch(N_SLOTS * NF).rearrange("p (s f) -> p s f", s=N_SLOTS)
        picked = scratch(BT * 2 * NF).rearrange("p (t s f) -> p t s f", t=BT, s=2)
        rows_f = scratch(BT * 2).rearrange("p (t s) -> p t s", t=BT)
        quadrant = scratch(1)
        q_ids_i = scratch(BT * Q * NF, I32).rearrange("p (t f) -> p t f", f=NF)
        q_ids_f = scratch(BT * Q * NF).rearrange("p (t f) -> p t f", f=NF)
        q_picked = scratch(BT * Q * (N_SLOTS - 2) * NF).rearrange("p (t s f) -> p t s f", f=NF, s=N_SLOTS - 2)
        q_rows_f = scratch(BT * Q * (N_SLOTS - 2)).rearrange("p (t s) -> p t s", s=N_SLOTS - 2)
        is_not = scratch(3 * N_SLOTS).rearrange("p (a s) -> p a s", a=3)
        paired = scratch(NF)
        remains = scratch(NF)
        no_not = scratch(NF)
        pair_of = scratch(2 * N_SLOTS * NF).rearrange("p (a s f) -> p a s f", a=2, s=N_SLOTS)
        other = scratch(4)
        bias_raw = scratch(P)
        assert used[0] <= KT * B
        dense_nat = nat[:, 4, 0:BT * P].rearrange("p (t d) -> p t d", t=BT)
        dense_w = nat[:, 5, 0:T1]
        TAIL_W, TAIL_X = KT - 2, KT - 1
        top_out = tanh_out[:, 1, 0:M2, :]
        y_row = tanh_out[0:1, 1, M2, :]

        mm = ctx.enter_context(nc.psum_tensor("mm", [P, 2, 2, B], F32))
        tp = ctx.enter_context(nc.psum_tensor("tp", [P, 2, KT, P], F32))
        quarters = table.rearrange("r (i c) -> (r i) c", i=Q)

        def raw_buf(u):
            return u % 2

        def turned_buf(u):
            n = (u - U_PAIR) % N_TURNED
            if n >= N_TURNED - 2:
                return tp[:, n - (N_TURNED - 2), :, :]
            return nat[:, 2 + n, :].rearrange("p (k b) -> p k b", k=KT)

        def by_tile(rows):
            return rows.rearrange("p (c k) -> p k c", k=KT)

        rem_dram = nc.dram_tensor("rem_dram", [P, BT, H], F32, kind="Internal").ap()

        ids_in = sem("ids_in")
        fields_in = sem("fields_in")
        first_in = sem("first_in")
        q_ids_in = sem("q_ids_in")
        bias_in = sem("bias_in")
        dense_in = sem("dense_in")
        dense_w_in = sem("dense_w_in")
        nat_in = [sem(f"nat_in{n}") for n in range(N_NAT)]
        rem_in = [sem(f"rem_in{n}") for n in range(BT)]
        raw_in = [sem(f"raw_in{n}") for n in range(N_RAW)]
        numbered = sem("numbered")
        ident_made = sem("ident_made")
        setup_step = sem("setup_step")
        rows_ready = sem("rows_ready")
        flags_ready = sem("flags_ready")
        bias_turned = sem("bias_turned")
        bias_ready = sem("bias_ready")
        rem_used = sem("rem_used")
        rem_stored = sem("rem_stored")
        rem_back = sem("rem_back")
        rem_turned = sem("rem_turned")
        rem_mixed = sem("rem_mixed")
        tail_zeroed = sem("tail_zeroed")
        tail_turned = sem("tail_turned")
        tail_hi = sem("tail_hi")
        tail_ready = sem("tail_ready")
        w_hi_ready = sem("w_hi_ready")
        w_ready = sem("w_ready")
        w_used = sem("w_used")
        transposed = sem("transposed")
        turned = sem("turned")
        fill_hi = sem("fill_hi")
        filled = sem("filled")
        pair_hi = sem("pair_hi")
        pair_lo = sem("pair_lo")
        act_step = sem("act_step")
        evac_act = sem("evac_act")
        and_hi = sem("and_hi")
        and_ready = sem("and_ready")
        mix_step = sem("mix_step")
        mix_sum = sem("mix_sum")
        evacuated = sem("evacuated")
        y_done = sem("y_done")
        y_ready = sem("y_ready")
        stored = sem("stored")

        block = ctx.enter_context(nc.Block())

        @block.sync
        def _(sp):
            def granule(w, k_tile, m, g, q):
                if not (isinstance(g, int) and g < N_RAW):
                    sp.wait_ge(w_ready, g - N_RAW + 1)
                src = w[k_tile * P:(k_tile + KG) * P, bass.ds(m * P, P)].rearrange("(k p) n -> p k n", p=P)
                sp.dma_start(w_raw[:, q, :, :], src).then_inc(raw_in[q], 16)

            def two_steps(parts, g0, i):
                for n in range(2 * len(parts)):
                    half, part = divmod(n, len(parts))
                    w, k_tile = parts[part]
                    granule(w, k_tile, i * 2 + half, i * (2 * len(parts)) + (g0 + n), (g0 + n) % N_RAW)

            not1 = [(Wn1, 0), (Wn1, KG)]
            two_steps(not1, G_NOT1, 0)
            with sp.Fori(1, KT // 2) as i:
                two_steps(not1, G_NOT1, i)
            with sp.Fori(0, KT // 2) as i:
                two_steps([(Wn2, 0), (Wn2, KG)], G_NOT2, i)
            for n in range(8):
                granule(Wa1, (n // 4 * 2 + n % 2) * KG, n // 2 % 2, G_AND1 + n, (G_AND1 + n) % N_RAW)
            with sp.Fori(1, KT // 2) as i:
                two_steps([(Wa1, n * KG) for n in range(4)], G_AND1, i)
            with sp.Fori(0, KT // 2) as i:
                two_steps([(Wo1, n * KG) for n in range(4)], G_OR1, i)
            with sp.Fori(0, KT // 2) as i:
                two_steps([(Wa2, 0), (Wa2, KG), (Wo2, 0), (Wo2, KG)], G_MIX, i)
            with sp.Fori(0, M1 // 2) as i:
                two_steps([(Wt1, 0), (Wt1, KG)], G_TOP1, i)
            for m in range(M2):
                granule(Wt2, 0, m, G_TOP2 + m, (G_TOP2 + m) % N_RAW)
            sp.wait_ge(y_ready, 1)
            sp.dma_start(out.rearrange("b o -> o b"), y_row).then_inc(stored, 16)
            sp.wait_ge(stored, 16)

        @block.gpsimd
        def _(pool):
            pool.iota(field_no_i, pattern=[[1, NF]], base=0, channel_multiplier=0).then_inc(numbered, 1)
            pool.memset(ident[:, :], 0.0).then_inc(ident_made, 1)
            pool.wait_ge(ident_made, 1)
            pool.affine_select(out=ident[:, :], in_=ident[:, :], compare_op=ALU.not_equal, fill=1.0, base=0,
                               pattern=[[-1, P]], channel_multiplier=1).then_inc(ident_made, 1)


            def gather(rows, tab, index, signal):
                pool.indirect_dma_start(rows, None, tab,
                                        bass.IndirectOffsetOnAxis(ap=index, axis=0)).then_inc(signal, 16)

            def gather_quarters(u):
                slot, bt = divmod(u, BT)
                if u < U_PAIR + 2:
                    pool.wait_ge(transposed, U_PAIR)
                else:
                    pool.wait_ge(turned, u - U_PAIR - 1)
                for g in range(Q):
                    n = bt * Q + g
                    gather(nat[:, raw_buf(u), g * (H // Q):(g + 1) * (H // Q)], quarters,
                           quarter_rows[:, n, slot - 2:slot - 1], nat_in[raw_buf(u)])

            pool.wait_ge(rows_ready, 1)
            for u in range(U_PAIR):
                slot, bt = divmod(u, BT)
                if u >= N_NAT:
                    pool.wait_ge(transposed, u - N_NAT + 1)
                gather(nat[:, u % N_NAT, :], table, rows_i[:, bt, slot:slot + 1], nat_in[u % N_NAT])
            pool.wait_ge(rows_ready, 2)
            for f in range(NF):
                for bt in range(BT):
                    if f:
                        pool.wait_ge(rem_used, (f - 1) * BT + bt + 1)
                    gather(rem_rows[:, bt, :], table, field_rows_i[:, bt, f:f + 1], rem_in[bt])
                if f == 0:
                    pool.wait_ge(rows_ready, 3)
                    gather_quarters(U_PAIR)
                    gather_quarters(U_PAIR + 1)
            for u in range(U_PAIR + 2, U_REM):
                gather_quarters(u)
                bt = u - (U_PAIR + 5)
                if 0 <= bt < BT:
                    pool.wait_ge(rem_used, (NF - 1) * BT + bt + 1)
                    pool.dma_start(rem_dram[:, bt, :], rem_sum[:, bt, :]).then_inc(rem_stored, 16)
            pool.wait_ge(filled, U_REM)
            pool.wait_ge(rem_stored, 16 * BT)
            for i in range(Q):
                pool.dma_start(
                    nat[i * R:(i + 1) * R, 0:BT, :].rearrange("r t (g c) -> r t g c", g=Q),
                    rem_dram[:, :, i * (H // Q):(i + 1) * (H // Q)].rearrange("(g r) t c -> r t g c", g=Q),
                ).then_inc(rem_back, 16)
            pool.memset(nat[:, BT:BT + 2, 0:B], 0.0).then_inc(tail_zeroed, 1)
            pool.wait_ge(tail_zeroed, 1)
            pool.dma_start(dense_nat[:, :, 0:ND], dense.rearrange("(t p) d -> p t d", p=P)).then_inc(dense_in, 16)
            pool.dma_start(dense_w[0:ND, :], Wt1[H:H + ND, :]).then_inc(dense_w_in, 16)

        @block.tensor
        def _(pe):
            def transpose_rows(rows, n):
                for k in range(KT):
                    last = pe.transpose(tp[:, n % 2, k, :], by_tile(rows)[:, k, :], ident[:, :])
                last.then_inc(transposed, 1)

            def transpose_not(u):
                pe.wait_ge(nat_in[u % N_NAT], 16 * (u // N_NAT + 1))
                if u >= 2:
                    pe.wait_ge(filled, u - 1)
                transpose_rows(nat[:, u % N_NAT, :], u)

            def products(bank, wh, wl, x, k, first, last):
                for j, buf in enumerate(x):
                    pe.matmul(bank[:, j, :], wh, x_hi[:, buf, k, :], start=first, stop=False)
                    pe.matmul(bank[:, j, :], wh, x_lo[:, buf, k, :], start=False, stop=False)
                for j, buf in enumerate(x):
                    ins = pe.matmul(bank[:, j, :], wl, x_hi[:, buf, k, :], start=False, stop=last)
                return ins

            def step(t, g, parity, operands, before=None, q0=0, dense_m=None):
                bank = mm[:, parity, :, :]
                pe.wait_ge(evacuated, t - 1) if not (isinstance(t, int) and t < 2) else None
                if dense_m is not None:
                    pe.wait_ge(tail_ready, 2)
                    cols = slice(dense_m * P, (dense_m + 1) * P)
                    products(bank, x_hi[:, 1, TAIL_W, cols], x_lo[:, 1, TAIL_W, cols], (1,), TAIL_X, True, False)
                n = sum(size for _, size in operands)
                tiles = [(x, k) for x, size in operands for k in range(size)]
                for at, (x, k) in enumerate(tiles):
                    if at % KG == 0:
                        pe.wait_ge(w_ready, g + at // KG + 1)
                    if before and at in before:
                        pe.wait_ge(*before[at])
                    q = (q0 + at // KG) % N_SPLIT
                    ins = products(bank, w_hi[:, q, at % KG, :], w_lo[:, q, at % KG, :], x, k,
                                   at == 0 and dense_m is None, at == n - 1)
                    if at % KG == KG - 1:
                        ins.then_inc(w_used, 1)

            def stage(t0, g0, operands, first, last, before=None):
                granules = sum(size for _, size in operands) // KG
                with pe.Fori(first, last) as i:
                    for half in range(2):
                        step(i * 2 + (t0 + half), i * (2 * granules) + (g0 + half * granules), half, operands, before)

            pe.wait_ge(bias_in, 16)
            pe.wait_ge(ident_made, 2)
            pe.transpose(mm[:, 1, 0, 0:N_BIAS], bias_raw[0:N_BIAS, :], ident[0:N_BIAS, 0:N_BIAS]).then_inc(bias_turned, 1)

            for u in range(BT):
                transpose_not(u)
            for x in range(2):
                pe.wait_ge(filled, (x + 1) * BT)
                for k in range(KT):
                    q, kk = divmod(k, KG)
                    pe.wait_ge(w_ready, q + 1)
                    ins = products(mm[:, 0, x:x + 1, :], w_hi[:, q, kk, :], w_lo[:, q, kk, :], (x,), k,
                                   k == 0, k == KT - 1)
                    if x == 1 and kk == KG - 1:
                        ins.then_inc(w_used, 1)
                    if x == 0 and k % 2 == 0:
                        transpose_not(BT + k // 2)
            nots = [((0, 1), KT)]
            pe.wait_ge(bias_ready, 1)
            step(1, G_NOT1 + 2, 1, nots)
            stage(S_NOT1, G_NOT1, nots, 1, KT // 2)
            stage(S_NOT2, G_NOT2, [((2, 3), KT)], 0, KT // 2, {KT - 1: (evacuated, S_NOT2)})

            for n in range(4):
                half, parity = divmod(n, 2)
                if half == 0:
                    pe.wait_ge(evacuated, S_AND1 + parity - 1)
                elif parity == 0:
                    pe.wait_ge(filled, U_PAIR + 4 * BT)
                for k in range(KT):
                    g, kk = G_AND1 + 2 * n + k // KG, k % KG
                    pe.wait_ge(w_ready, g + 1) if kk == 0 else None
                    pe.wait_ge(pair_lo, 2 * k + 2) if n == 0 else None
                    ins = products(mm[:, parity, :, :], w_hi[:, g % N_SPLIT, kk, :], w_lo[:, g % N_SPLIT, kk, :],
                                   (2 * half, 2 * half + 1), k, half == 0 and k == 0, half == 1 and k == KT - 1)
                    if kk == KG - 1:
                        ins.then_inc(w_used, 1)
            stage(S_AND1, G_AND1, [((0, 1), KT), ((2, 3), KT)], 1, KT // 2)

            stage(S_OR1, G_OR1, [((0,), KT), ((1,), KT)], 0, KT // 2,
                  {0: (filled, U_REM - BT), KT: (filled, U_REM)})

            mixed = [((2,), KT), ((3,), KT)]
            before = {KT - 1: (and_ready, KT), 2 * KT - 1: (evacuated, S_MIX)}
            step(S_MIX, G_MIX, 0, mixed, before)
            pe.wait_ge(dense_in, 16)
            pe.wait_ge(rem_mixed, BT)
            for bt in range(BT):
                last = pe.transpose(tp[:, 0, bt, :], dense_nat[:, bt, :], ident[:, :])
            last.then_inc(tail_turned, 1)
            step(S_MIX + 1, G_MIX + 4, 1, mixed, before)
            stage(S_MIX, G_MIX, mixed, 1, KT // 2, before)

            for m in range(M1):
                step(S_TOP1 + m, G_TOP1 + 2 * m, m % 2, [((0,), KT)], {KT - 1: (evacuated, S_TOP1)}, dense_m=m)
            for m in range(M2):
                step(S_TOP2 + m, G_TOP2 + m, m % 2, [((1,), KG)], {KG - 1: (evacuated, S_TOP2)}, q0=m)
            for m in range(M2):
                pe.wait_ge(evac_act, S_TOP2 + m + 1)
                last = pe.matmul(mm[0:1, 0, 0, :], bias[:, C_W3 + m:C_W3 + m + 1], top_out[:, m, :],
                                 start=m == 0, stop=m == M2 - 1)
            last.then_inc(y_done, 1)

        def column(c, m):
            return bias[:, bass.ds(m + c, 1)]

        def tile(t, m):
            return t[:, bass.ds(m, 1), :].rearrange("p k b -> p (k b)")

        def load_flags(engine):
            engine.wait_ge(flags_ready, 1)
            return ({s: engine.value_load(flags[0:1, a, s:s + 1], min_val=0, max_val=1) for s in range(2, N_SLOTS)}
                    for a in range(2))

        @block.scalar
        def _(act):
            act.dma_start(ids_i, ids.rearrange("(t p) f -> p t f", p=P)).then_inc(ids_in, 16)
            act.dma_start(fields_i, fields.partition_broadcast(P)).then_inc(fields_in, 16)
            act.dma_start(first_i, first_row.partition_broadcast(P)).then_inc(first_in, 16)
            act.dma_start(bias_raw[0:N_BIAS, :], bias_rows).then_inc(bias_in, 16)
            for i in range(Q):
                act.dma_start(q_ids_i[i * R:(i + 1) * R, :, :],
                              ids.rearrange("(t r) f -> r t f", r=R)).then_inc(q_ids_in, 16)

            def split(c, i=0, per=0):
                g = i * per + c
                act.wait_ge(raw_in[c % N_RAW], i * (16 * (per // N_RAW)) + 16 * (c // N_RAW + 1))
                if c >= N_SPLIT:
                    act.wait_ge(w_used, g - N_SPLIT + 1)
                act.activation(w_hi[:, c % N_SPLIT, :, :], w_raw[:, c % N_RAW, :, :], ACT.Copy).then_inc(w_hi_ready, 1)

            idle = iter(range(idle_act.shape[1]))

            def nothing(signal):
                n = next(idle)
                act.activation(idle_act[:, n:n + 1], ident[:, 0:1], ACT.Copy).then_inc(signal, 1)

            def fill(u, buf):
                slot, bt = divmod(u, BT)
                to = x_hi[:, buf, :, bt * P:(bt + 1) * P]
                if slot < 2:
                    act.wait_ge(transposed, u + 1)
                    act.activation(to, tp[:, u % 2, :, :], ACT.Copy).then_inc(fill_hi, 1)
                    return
                act.wait_ge(turned, u - U_PAIR + 1)
                if slot < 4:
                    with act.If(is_not_field[slot] == 0):
                        act.activation(to, turned_buf(u), ACT.Copy).then_inc(fill_hi, 1)
                    with act.Else():
                        nothing(fill_hi)
                    return
                with act.If(is_not_field[slot] == 0):
                    act.activation(to, turned_buf(u), ACT.Copy).then_inc(fill_hi, 1)
                with act.Else():
                    of = tanh_out[:, bass.ds(which_not[slot], 1), :, bt * P:(bt + 1) * P]
                    act.activation(to, of.rearrange("p a k b -> p (a k) b"), ACT.Copy).then_inc(fill_hi, 1)

            def to_hidden(bufs, c):
                def evac(m, t, parity):
                    n = len(bufs)
                    for j in range(n):
                        act.activation(mm[:, parity, j, :], mm[:, parity, j, :], ACT.Relu,
                                       bias=column(c, m)).then_inc(act_step, 1)
                    act.wait_ge(act_step, act_base[c] + m * n + n)
                    for j, buf in enumerate(bufs):
                        last = act.activation(tile(x_hi[:, buf, :, :], m), mm[:, parity, j, :], ACT.Copy)
                    last.then_inc(evac_act, 1)
                return evac

            act_base = {C_N1: 0, C_O1: 2 * KT, C_T1: 3 * KT}

            def not2_evac(m, t, parity):
                act.wait_ge(rem_used, NF * BT)
                for j in range(2):
                    last = act.activation(tile(tanh_out[:, j, :, :], m), mm[:, parity, j, :], ACT.Tanh,
                                          bias=column(C_N2, m))
                last.then_inc(evac_act, 1)
                act.wait_ge(evac_act, t + 1)
                for buf in range(2):
                    with act.If(is_not_field[2 + buf] == 1):
                        of = tanh_out[:, bass.ds(which_not[2 + buf], 1), m, :]
                        act.activation(x_hi[:, buf, m, :], of.rearrange("p a b -> p (a b)"), ACT.Copy).then_inc(pair_hi, 1)
                    with act.Else():
                        nothing(pair_hi)

            def and_evac(m, t, parity):
                act.activation(tile(and_hidden, m), mm[:, parity, 0, :], ACT.Relu, bias=column(C_A1, m))
                act.activation(mm[:, parity, 1, :], mm[:, parity, 1, :], ACT.Relu,
                               bias=column(C_A1, m)).then_inc(evac_act, 1)

            def or_evac(m, t, parity):
                act.activation(tile(x_hi[:, 2, :, :], m), tile(and_hidden, m), ACT.Copy).then_inc(and_hi, 1)
                to_hidden((3,), C_O1)(m, t, parity)

            def mix_evac(m, t, parity):
                act.wait_ge(mix_sum, m + 1)
                act.activation(tile(x_hi[:, 0, :, :], m), tile(tanh_out[:, 0, :, :], m), ACT.Copy,
                               scale=one_by_count[:, 0:1]).then_inc(evac_act, 1)

            def step(i, half, t0, g0, granules, evac):
                per = 2 * granules
                c = g0 + half * granules
                for n in range(2, granules + 2):
                    split(c + n, i, per)
                act.wait_ge(w_used, i * per + c + granules)
                evac(i * 2 + half, i * 2 + (t0 + half), half)

            def stage(t0, g0, granules, evac, first=0, last=KT // 2):
                with act.Fori(first, last) as i:
                    for half in range(2):
                        step(i, half, t0, g0, granules, evac)

            split(0)
            split(1)
            for u in range(2 * BT):
                fill(u, u // BT)
            act.wait_ge(bias_ready, 1)
            step(0, 0, S_NOT1, G_NOT1, 2, to_hidden((2, 3), C_N1))
            step(0, 1, S_NOT1, G_NOT1, 2, to_hidden((2, 3), C_N1))
            is_not_field, which_not = load_flags(act)
            stage(S_NOT1, G_NOT1, 2, to_hidden((2, 3), C_N1), 1)
            for m in range(KT):
                c = G_NOT2 + 2 * m
                split(c + 2)
                split(c + 3)
                act.wait_ge(w_used, c + 2)
                not2_evac(m, S_NOT2 + m, m % 2)
                for u in range(U_PAIR + 2 * m, U_PAIR + 2 * m + 2) if m < BT else ():
                    fill(u, u // BT - 2)
            fill(16, 2), fill(17, 2)
            split(G_AND1 + 2)
            fill(18, 2), fill(19, 2)
            split(G_AND1 + 3)
            fill(20, 3), fill(21, 3), fill(22, 3), fill(23, 3)
            for n in range(4, 7):
                split(G_AND1 + n)
            act.wait_ge(w_used, G_AND1 + 6)
            act.wait_ge(rem_stored, 16 * BT)
            and_evac(0, S_AND1, 0)
            for n in range(7, 10):
                split(G_AND1 + n)
            act.wait_ge(w_used, G_AND1 + 8)
            and_evac(1, S_AND1 + 1, 1)
            stage(S_AND1, G_AND1, 4, and_evac, 1, KT // 2 - 1)
            step(KT // 2 - 1, 0, S_AND1, G_AND1, 4, and_evac)
            split(G_OR1 - 2)
            split(G_OR1 - 1)
            act.wait_ge(w_used, G_OR1 - 2)
            fill(24, 0), fill(25, 0), fill(26, 0), fill(27, 0)
            split(G_OR1)
            fill(28, 1)
            split(G_OR1 + 1)
            fill(29, 1), fill(30, 1), fill(31, 1)
            act.wait_ge(w_used, G_OR1)
            and_evac(KT - 1, S_OR1 - 1, 1)
            stage(S_OR1, G_OR1, 4, or_evac)

            step(0, 0, S_MIX, G_MIX, 4, mix_evac)
            act.wait_ge(tail_turned, 1)
            act.activation(x_hi[:, 1, TAIL_X, :], tp[:, 0, 0:BT, :].rearrange("p t b -> p (t b)"),
                           ACT.Copy).then_inc(tail_hi, 1)
            act.wait_ge(dense_w_in, 16)
            act.activation(x_hi[:, 1, TAIL_W, :], dense_w, ACT.Copy).then_inc(tail_hi, 1)
            step(0, 1, S_MIX, G_MIX, 4, mix_evac)
            stage(S_MIX, G_MIX, 4, mix_evac, 1)

            for m in range(M1):
                c = G_TOP1 + 2 * m
                split(c + 2)
                split(c + 3)
                act.wait_ge(w_used, c + 2)
                to_hidden((1,), C_T1)(m, S_TOP1 + m, m % 2)
            for m in range(M2):
                act.wait_ge(w_used, G_TOP2 + m + 1)
                act.activation(top_out[:, m, :], mm[:, m, 0, :], ACT.Relu, bias=column(C_T2, m)).then_inc(evac_act, 1)
            act.wait_ge(y_done, 1)
            act.activation(y_row, mm[0:1, 0, 0, :], ACT.Copy).then_inc(y_ready, 1)

        @block.vector
        def _(dve):
            done = [0]

            def link(ins):
                done[0] += 1
                ins.then_inc(setup_step, 1)
                dve.wait_ge(setup_step, done[0])

            dve.wait_ge(fields_in, 16)
            dve.wait_ge(numbered, 1)
            dve.tensor_copy(fields_f, fields_i).then_inc(setup_step, 1)
            dve.tensor_copy(field_no, field_no_i).then_inc(setup_step, 1)
            dve.wait_ge(ids_in, 16)
            dve.wait_ge(first_in, 16)
            dve.tensor_copy(ids_f, ids_i).then_inc(setup_step, 1)
            done[0] = 3
            link(dve.tensor_copy(first_f, first_i))
            dve.tensor_tensor(ids_f, ids_f, first_f.unsqueeze(1).to_broadcast([P, BT, NF]), ALU.add).then_inc(setup_step, 1)
            done[0] = 5
            link(dve.tensor_tensor(is_field, fields_f.unsqueeze(2).to_broadcast([P, N_SLOTS, NF]),
                                   field_no.unsqueeze(1).to_broadcast([P, N_SLOTS, NF]), ALU.is_equal))
            link(dve.tensor_tensor(picked, is_field[:, 0:2, :].unsqueeze(1).to_broadcast([P, BT, 2, NF]),
                                   ids_f.unsqueeze(2).to_broadcast([P, BT, 2, NF]), ALU.mult))
            link(dve.tensor_reduce(rows_f, picked, AX.X, ALU.add))
            dve.tensor_copy(rows_i[:, :, :], rows_f).then_inc(rows_ready, 1)
            dve.tensor_copy(field_rows_i[:, :, :], ids_f).then_inc(rows_ready, 1)

            def split(c, i=0, per=0):
                dve.wait_ge(w_hi_ready, i * per + c + 1)
                dve.tensor_tensor(w_lo[:, c % N_SPLIT, :, :], w_raw[:, c % N_RAW, :, :],
                                  w_hi[:, c % N_SPLIT, :, :].bitcast(F32), ALU.subtract).then_inc(w_ready, 1)

            def turn(u):
                n = u - U_PAIR
                dve.wait_ge(nat_in[raw_buf(u)], 16 * X_USES[raw_buf(u)] + 16 * Q * (n // 2 + 1))
                if n >= N_TURNED:
                    dve.wait_ge(filled, u - N_TURNED + 1)
                dve.transpose(turned_buf(u).rearrange("p k (g r) -> p g k r", g=Q),
                              nat[:, raw_buf(u), :].rearrange("p (g c k) -> p g k c", g=Q, k=KT)).then_inc(turned, 1)

            idle = iter(range(idle_dve.shape[1]))

            def nothing(signal):
                n = next(idle)
                dve.memset(idle_dve[:, n:n + 1], 0.0).then_inc(signal, 1)

            def fill(u, buf):
                slot, bt = divmod(u, BT)
                cols = slice(bt * P, (bt + 1) * P)
                to, hi = x_lo[:, buf, :, cols], x_hi[:, buf, :, cols].bitcast(F32)
                dve.wait_ge(fill_hi, u + 1)
                if slot < 2:
                    dve.tensor_tensor(to, tp[:, u % 2, :, :], hi, ALU.subtract).then_inc(filled, 1)
                    return
                if slot < 4:
                    with dve.If(is_not_field[slot] == 0):
                        dve.tensor_tensor(to, turned_buf(u), hi, ALU.subtract).then_inc(filled, 1)
                    with dve.Else():
                        nothing(filled)
                    return
                with dve.If(is_not_field[slot] == 0):
                    dve.tensor_tensor(to, turned_buf(u), hi, ALU.subtract).then_inc(filled, 1)
                with dve.Else():
                    of = tanh_out[:, bass.ds(which_not[slot], 1), :, cols].rearrange("p a k b -> p (a k) b")
                    dve.tensor_tensor(to, of, hi, ALU.subtract).then_inc(filled, 1)

            def lo_part(buf, m, src):
                return dve.tensor_tensor(tile(x_lo[:, buf, :, :], m), src,
                                         tile(x_hi[:, buf, :, :], m).bitcast(F32), ALU.subtract)

            def to_hidden(bufs):
                def evac(m, t, parity):
                    dve.wait_ge(evac_act, t + 1)
                    for j, buf in enumerate(bufs):
                        last = lo_part(buf, m, mm[:, parity, j, :])
                    last.then_inc(evacuated, 1)
                return evac

            def not2_evac(m, t, parity):
                dve.wait_ge(evac_act, t + 1)
                dve.sem_inc(evacuated, 1)
                for buf in range(2):
                    dve.wait_ge(pair_hi, 2 * m + buf + 1)
                    with dve.If(is_not_field[2 + buf] == 1):
                        of = tanh_out[:, bass.ds(which_not[2 + buf], 1), m, :]
                        dve.tensor_tensor(x_lo[:, buf, m, :], of.rearrange("p a b -> p (a b)"),
                                          x_hi[:, buf, m, :].bitcast(F32), ALU.subtract).then_inc(pair_lo, 1)
                    with dve.Else():
                        nothing(pair_lo)

            def and_evac(m, t, parity):
                dve.wait_ge(evac_act, t + 1)
                dve.tensor_tensor(tile(and_hidden, m), tile(and_hidden, m), mm[:, parity, 1, :],
                                  ALU.add).then_inc(evacuated, 1)

            def or_evac(m, t, parity):
                t0, t1 = tile(tanh_out[:, 0, :, :], m), tile(tanh_out[:, 1, :, :], m)
                dve.tensor_scalar(t0, t0, rem_t[:, 0:1], None, ALU.mult).then_inc(mix_step, 1)
                dve.wait_ge(and_hi, m + 1)
                lo_part(2, m, tile(and_hidden, m)).then_inc(and_ready, 1)
                dve.wait_ge(mix_step, m + 1)
                dve.scalar_tensor_tensor(t0, t1, rem_t[:, 1:2], t0, ALU.mult, ALU.add)
                to_hidden((3,))(m, t, parity)

            def mix_evac(m, t, parity):
                z = tile(tanh_out[:, 0, :, :], m)
                dve.wait_ge(w_used, mix_used(m))
                dve.scalar_tensor_tensor(z, mm[:, parity, 0, :], mix_bias[:, bass.ds(m, 1)], z, ALU.add,
                                         ALU.add).then_inc(mix_sum, 1)
                dve.wait_ge(evac_act, t + 1)
                dve.scalar_tensor_tensor(tile(x_lo[:, 0, :, :], m), z, one_by_count[:, 0:1],
                                         tile(x_hi[:, 0, :, :], m).bitcast(F32), ALU.mult,
                                         ALU.subtract).then_inc(evacuated, 1)

            def mix_used(m):
                return m * 4 + (G_MIX + 4)

            def step(i, half, t0, g0, granules, evac):
                per = 2 * granules
                c = g0 + half * granules
                for n in range(2, granules + 2):
                    split(c + n, i, per)
                evac(i * 2 + half, i * 2 + (t0 + half), half)

            def stage(t0, g0, granules, evac, first=0, last=KT // 2):
                with dve.Fori(first, last) as i:
                    for half in range(2):
                        step(i, half, t0, g0, granules, evac)

            def not1_evac(m, t, parity):
                to_hidden((2, 3))(m, t, parity)
                if not isinstance(m, int) or m:
                    dve.wait_ge(rem_used, m * BT)
                for bt in range(BT):
                    dve.wait_ge(rem_in[bt], m * 16 + 16)
                    if isinstance(m, int) and m == 0:
                        dve.tensor_scalar(rem_sum[:, bt, :], rem_rows[:, bt, :], rem_e[:, 0:1], None,
                                          ALU.mult).then_inc(rem_used, 1)
                        continue
                    dve.scalar_tensor_tensor(rem_sum[:, bt, :], rem_rows[:, bt, :], rem_e[:, bass.ds(m, 1)],
                                             rem_sum[:, bt, :], ALU.mult, ALU.add).then_inc(rem_used, 1)

            split(0)
            split(1)
            for u in range(BT):
                fill(u, 0)

            NS = N_SLOTS - 2
            dve.wait_ge(q_ids_in, 16 * Q)
            for i in range(Q):
                dve.memset(quadrant[i * R:(i + 1) * R, :], float(i)).then_inc(setup_step, 1)
            done[0] += Q
            link(dve.tensor_copy(q_ids_f, q_ids_i))
            link(dve.tensor_tensor(q_ids_f, q_ids_f, first_f.unsqueeze(1).to_broadcast([P, BT * Q, NF]), ALU.add))
            link(dve.tensor_tensor(q_picked, is_field[:, 2:N_SLOTS, :].unsqueeze(1).to_broadcast([P, BT * Q, NS, NF]),
                                   q_ids_f.unsqueeze(2).to_broadcast([P, BT * Q, NS, NF]), ALU.mult))
            link(dve.tensor_reduce(q_rows_f, q_picked, AX.X, ALU.add))
            dve.tensor_scalar(quarter_rows[:, :, :], q_rows_f, float(Q), quadrant[:, 0:1], ALU.mult,
                              ALU.add).then_inc(rows_ready, 1)

            link(dve.tensor_reduce(paired, is_field[:, 2:N_SLOTS, :].rearrange("p s f -> p f s"), AX.X, ALU.max))
            link(dve.tensor_scalar(remains, paired, -1.0, 1.0, ALU.mult, ALU.add))
            link(dve.tensor_reduce(other[:, 0:1], remains, AX.X, ALU.add))
            link(dve.tensor_scalar(other[:, 0:1], other[:, 0:1], float((N_SLOTS - 2) // 2), None, ALU.add))
            dve.reciprocal(one_by_count[:, :], other[:, 0:1]).then_inc(setup_step, 1)
            done[0] += 1
            link(dve.tensor_tensor(no_not, is_field[:, 0, :], is_field[:, 1, :], ALU.max))
            link(dve.tensor_scalar(no_not, no_not, -1.0, 1.0, ALU.mult, ALU.add))
            link(dve.tensor_tensor(rem_e[:, :], remains, no_not, ALU.mult))
            for a in range(2):
                last = dve.tensor_tensor(pair_of[:, a, :, :], is_field,
                                         is_field[:, a, :].unsqueeze(1).to_broadcast([P, N_SLOTS, NF]), ALU.mult)
            link(last)
            link(dve.tensor_reduce(is_not[:, 0:2, :], pair_of, AX.X, ALU.add))
            dve.tensor_tensor(flags[:, 0, :], is_not[:, 0, :], is_not[:, 1, :], ALU.max).then_inc(setup_step, 1)
            done[0] += 1
            link(dve.tensor_scalar(flags[:, 1, :], is_not[:, 0, :], -1.0, 1.0, ALU.mult, ALU.add))
            link(dve.tensor_tensor(pair_of[:, 0, 0:2, :], is_field[:, 0:2, :],
                                   remains.unsqueeze(1).to_broadcast([P, 2, NF]), ALU.mult))
            link(dve.tensor_reduce(rem_t[:, :], pair_of[:, 0, 0:2, :], AX.X, ALU.add))
            link(dve.tensor_scalar(other[:, 1:2], is_not[:, 0, 1:2], -1.0, 1.0, ALU.mult, ALU.add))
            link(dve.tensor_tensor(rem_t[:, 1:2], rem_t[:, 1:2], other[:, 1:2], ALU.mult))
            dve.sem_inc(flags_ready, 1)

            dve.wait_ge(bias_turned, 1)
            link(dve.tensor_copy(bias[:, :], mm[:, 1, 0, 0:N_BIAS]))
            dve.scalar_tensor_tensor(mix_bias[:, :], bias[:, C_A2:C_A2 + KT], 2.0, bias[:, C_O2:C_O2 + KT],
                                     ALU.mult, ALU.add).then_inc(bias_ready, 1)

            for u in range(BT, 2 * BT):
                fill(u, 1)
            step(0, 0, S_NOT1, G_NOT1, 2, not1_evac)
            step(0, 1, S_NOT1, G_NOT1, 2, not1_evac)
            is_not_field, which_not = load_flags(dve)
            stage(S_NOT1, G_NOT1, 2, not1_evac, 1)
            turn_at = [(8, 9), (10, 11), (12, 13), (14, 15), (16, 17), (18, 19), (20,), (21,)]
            for m in range(KT):
                split(G_NOT2 + 2 * m + 2)
                split(G_NOT2 + 2 * m + 3)
                not2_evac(m, S_NOT2 + m, m % 2)
                for u in turn_at[m]:
                    turn(u)
                for u in range(U_PAIR + 2 * m, U_PAIR + 2 * m + 2) if m < BT else ():
                    fill(u, u // BT - 2)
            fill(16, 2), fill(17, 2)
            split(G_AND1 + 2)
            turn(22)
            fill(18, 2), fill(19, 2)
            split(G_AND1 + 3)
            turn(23)
            fill(20, 3), fill(21, 3), fill(22, 3), fill(23, 3)
            for n in range(4, 7):
                split(G_AND1 + n)
            and_evac(0, S_AND1, 0)
            for n in range(7, 10):
                split(G_AND1 + n)
            and_evac(1, S_AND1 + 1, 1)
            turn(24)
            for m in range(2, KT - 1):
                step(m // 2, m % 2, S_AND1, G_AND1, 4, and_evac)
                turn(23 + m)
            split(G_OR1 - 2)
            split(G_OR1 - 1)
            fill(24, 0), fill(25, 0)
            turn(30)
            fill(26, 0), fill(27, 0)
            split(G_OR1)
            turn(31)
            fill(28, 1)
            split(G_OR1 + 1)
            fill(29, 1), fill(30, 1), fill(31, 1)
            and_evac(KT - 1, S_OR1 - 1, 1)
            dve.wait_ge(evacuated, S_OR1)
            stage(S_OR1, G_OR1, 4, or_evac)

            def turn_rem(bt):
                dve.transpose(tp[:, bt % 2, :, :].rearrange("p k (g r) -> p g k r", g=Q),
                              nat[:, bt, :].rearrange("p (g c k) -> p g k c", g=Q, k=KT)).then_inc(rem_turned, 1)

            def mix_rem(bt):
                part = tanh_out[:, 0, :, bt * P:(bt + 1) * P]
                dve.wait_ge(rem_turned, bt + 1)
                dve.tensor_tensor(part, part, tp[:, bt % 2, :, :], ALU.add).then_inc(rem_mixed, 1)

            dve.wait_ge(evacuated, S_MIX)
            dve.wait_ge(rem_back, 16 * Q)
            turn_rem(0), turn_rem(1)
            split(G_MIX + 2)
            mix_rem(0), mix_rem(1)
            split(G_MIX + 3)
            dve.wait_ge(rem_mixed, 2)
            turn_rem(2), turn_rem(3)
            split(G_MIX + 4)
            mix_rem(2), mix_rem(3)
            split(G_MIX + 5)
            dve.wait_ge(rem_mixed, BT)
            mix_evac(0, S_MIX, 0)
            dve.wait_ge(tail_hi, 1)
            dve.tensor_tensor(x_lo[:, 1, TAIL_X, :], tp[:, 0, 0:BT, :].rearrange("p t b -> p (t b)"),
                              x_hi[:, 1, TAIL_X, :].bitcast(F32), ALU.subtract).then_inc(tail_ready, 1)
            dve.wait_ge(tail_hi, 2)
            dve.tensor_tensor(x_lo[:, 1, TAIL_W, :], dense_w, x_hi[:, 1, TAIL_W, :].bitcast(F32),
                              ALU.subtract).then_inc(tail_ready, 1)
            step(0, 1, S_MIX, G_MIX, 4, mix_evac)
            stage(S_MIX, G_MIX, 4, mix_evac, 1)
            for m in range(M1):
                c = G_TOP1 + 2 * m
                split(c + 2) if c + 2 < G_TOP2 + M2 else None
                split(c + 3) if c + 3 < G_TOP2 + M2 else None
                to_hidden((1,))(m, S_TOP1 + m, m % 2)


def kernel(dense_ctx, ids, tbl_0, tbl_1, tbl_2, tbl_3, tbl_4, tbl_5, tbl_6, tbl_7, W_top1, b_top1, W_top2, b_top2,
           W_top3, L0_rec_Wn1, L0_rec_bn1, L0_rec_Wn2, L0_rec_bn2, L0_rec_Wa1, L0_rec_ba1, L0_rec_Wa2, L0_rec_ba2,
           L0_rec_Wo1, L0_rec_bo1, L0_rec_Wo2, L0_rec_bo2, L0_rec_not_idx, L0_rec_and_pairs, L0_rec_or_pairs):
    import numpy as np
    import concourse.bacc as bacc
    from concourse.bass_utils import run_bass_kernel_spmd

    tables = [tbl_0, tbl_1, tbl_2, tbl_3, tbl_4, tbl_5, tbl_6, tbl_7]
    sizes = [t.shape[0] for t in tables]
    H_TILES = tbl_0.shape[1] // P
    arrays = {
        "dense": dense_ctx,
        "ids": ids,
        "fields": np.concatenate([np.ravel(L0_rec_not_idx), np.ravel(np.transpose(L0_rec_and_pairs)),
                                  np.ravel(L0_rec_or_pairs)]),
        "table": np.concatenate(tables).reshape(-1, H_TILES, P).transpose(0, 2, 1).reshape(-1, H_TILES * P),
        "first_row": np.array([sum(sizes[:n]) for n in range(len(sizes))], np.int32),
        "Wn1": L0_rec_Wn1, "Wn2": L0_rec_Wn2, "Wa1": L0_rec_Wa1, "Wa2": L0_rec_Wa2,
        "Wo1": L0_rec_Wo1, "Wo2": L0_rec_Wo2, "Wt1": W_top1, "Wt2": W_top2,
        "bias_rows": np.concatenate([L0_rec_bn1, L0_rec_bn2, L0_rec_ba1, L0_rec_ba2, L0_rec_bo1, L0_rec_bo2,
                                     b_top1, b_top2, np.ravel(W_top3)]).reshape(-1, P),
    }
    arrays = {k: np.ascontiguousarray(v) for k, v in arrays.items()}
    nc = bacc.Bacc("TRN2", target_bir_lowering=False, num_devices=1, dynamic_dma_scratch_size=SCRATCH)
    aps = {k: nc.dram_tensor(k, v.shape, mybir.dt.from_np(v.dtype), kind="ExternalInput").ap()
           for k, v in arrays.items()}
    out = nc.dram_tensor("out", (ids.shape[0], 1), F32, kind="ExternalOutput").ap()
    logic_tower(nc, *aps.values(), out)
    return run_bass_kernel_spmd(nc, [arrays], core_ids=[0]).results[0]["out"]
```

```python
from contextlib import ExitStack

import concourse.bass as bass
from concourse import mybir

P = 128
F32 = mybir.dt.float32
F32R = mybir.dt.float32r
I32 = mybir.dt.int32
ALU = mybir.AluOpType
ACT = mybir.ActivationFunctionType
AX = mybir.AxisListType

SCRATCH = 4096
N_NAT = 6
N_RAW = 4
N_SPLIT = 2
KG = 4
N_SLOTS = 8

WARM_UP = 25
N_TURNED = 6
Q = 4
R = P // Q


def logic_tower(nc, dense, ids, fields, table, first_row, Wn1, Wn2, Wa1, Wa2, Wo1, Wo2, Wt1, Wt2, bias_rows, out):
    B, NF = ids.shape
    H = Wn1.shape[0]
    ND = dense.shape[1]
    T1, T2 = Wt1.shape[1], Wt2.shape[1]
    BT, KT = B // P, H // P
    M1, M2 = T1 // P, T2 // P
    N_BIAS = bias_rows.shape[0]
    assert B == 512 and KT == 2 * KG and M1 == KG and NF == 8 and ND <= R

    S_NOT1, S_NOT2, S_AND1, S_OR1, S_MIX, S_TOP1 = (n * KT for n in range(6))
    S_TOP2 = S_TOP1 + M1
    S_Y = S_TOP2 + M2
    G_NOT1, G_NOT2, G_AND1 = 0, 2 * KT, 4 * KT
    G_OR1, G_MIX, G_TOP1 = G_AND1 + 4 * KT, G_AND1 + 8 * KT, G_AND1 + 12 * KT
    G_TOP2 = G_TOP1 + 2 * M1
    C_N1, C_N2, C_A1, C_A2, C_O1, C_O2, C_T1 = (n * KT for n in range(7))
    C_T2 = C_T1 + M1
    C_W3 = C_T2 + M2
    assert N_BIAS == C_W3 + M2
    U_REM = N_SLOTS * BT
    U_PAIR = 2 * BT
    U_SECOND = 4 * BT
    U_OR = 6 * BT
    X_USES = [sum(u % N_NAT == n for u in range(U_PAIR)) for n in range(N_NAT)]

    with ExitStack() as ctx:
        def sb(name, shape, dt):
            return ctx.enter_context(nc.sbuf_tensor(name, shape, dt))

        def sem(name):
            return ctx.enter_context(nc.semaphore(name))

        x_hi = sb("x_hi", [P, 4, KT, B], F32R)
        x_lo = sb("x_lo", [P, 4, KT, B], F32R)
        tanh_out = sb("tanh_out", [P, 2, KT, B], F32)
        and_hidden = sb("and_hidden", [P, KT, B], F32)
        nat = sb("nat", [P, N_NAT, H], F32)
        w_raw = sb("w_raw", [P, N_RAW, KG, P], F32)
        w_hi = sb("w_hi", [P, N_SPLIT, KG, P], F32R)
        w_lo = sb("w_lo", [P, N_SPLIT, KG, P], F32R)
        ident = sb("ident", [P, P], F32)
        bias = sb("bias", [P, N_BIAS], F32)
        mix_bias = sb("mix_bias", [P, KT], F32)
        rows_i = sb("rows_i", [P, BT, 2], I32)
        quarter_rows = sb("quarter_rows", [P, BT * Q, N_SLOTS - 2], I32)
        field_rows_i = sb("field_rows_i", [P, BT, NF], I32)
        rem_e = sb("rem_e", [P, NF], F32)
        rem_t = sb("rem_t", [P, 2], F32)
        one_by_count = sb("one_by_count", [P, 1], F32)
        idle_act = sb("idle_act", [P, 2 * BT + 2 * KT], F32)
        idle_dve = sb("idle_dve", [P, 2 * BT + 2 * KT], F32)
        flags = sb("flags", [P, 2, N_SLOTS], I32)
        rem_rows = tanh_out[:, 0, :, :].rearrange("p k b -> p (k b)").rearrange("p (t h) -> p t h", t=BT)
        rem_sum = and_hidden[:, :, :].rearrange("p k b -> p (k b)").rearrange("p (t h) -> p t h", t=BT)
        setup = tanh_out[:, 1, :, :].rearrange("p k b -> p (k b)")
        used = [0]

        def scratch(n, dt=F32):
            at, used[0] = used[0], used[0] + n
            v = setup[:, at:at + n]
            return v if dt == F32 else v.bitcast(dt)

        ids_i = scratch(BT * NF, I32).rearrange("p (t f) -> p t f", t=BT)
        ids_f = scratch(BT * NF).rearrange("p (t f) -> p t f", t=BT)
        fields_i = scratch(N_SLOTS, I32)
        fields_f = scratch(N_SLOTS)
        first_i = scratch(NF, I32)
        first_f = scratch(NF)
        field_no_i = scratch(NF, I32)
        field_no = scratch(NF)
        is_field = scratch(N_SLOTS * NF).rearrange("p (s f) -> p s f", s=N_SLOTS)
        picked = scratch(BT * 2 * NF).rearrange("p (t s f) -> p t s f", t=BT, s=2)
        rows_f = scratch(BT * 2).rearrange("p (t s) -> p t s", t=BT)
        quadrant = scratch(1)
        q_ids_i = scratch(BT * Q * NF, I32).rearrange("p (t f) -> p t f", f=NF)
        q_ids_f = scratch(BT * Q * NF).rearrange("p (t f) -> p t f", f=NF)
        q_picked = scratch(BT * Q * (N_SLOTS - 2) * NF).rearrange("p (t s f) -> p t s f", f=NF, s=N_SLOTS - 2)
        q_rows_f = scratch(BT * Q * (N_SLOTS - 2)).rearrange("p (t s) -> p t s", s=N_SLOTS - 2)
        is_not = scratch(3 * N_SLOTS).rearrange("p (a s) -> p a s", a=3)
        paired = scratch(NF)
        remains = scratch(NF)
        no_not = scratch(NF)
        pair_of = scratch(2 * N_SLOTS * NF).rearrange("p (a s f) -> p a s f", a=2, s=N_SLOTS)
        other = scratch(4)
        bias_raw = scratch(P)
        assert used[0] <= KT * B
        dense_nat = nat[:, 4, 0:BT * P].rearrange("p (t d) -> p t d", t=BT)
        dense_w = nat[:, 5, 0:T1]
        TAIL_W, TAIL_X = KT - 2, KT - 1
        LO_X, LO_W = slice(R, 2 * R), slice(2 * R, 3 * R)
        top_out = tanh_out[:, 1, 0:M2, :]
        y_row = tanh_out[0:1, 1, M2, :]

        mm = ctx.enter_context(nc.psum_tensor("mm", [P, 2, 2, B], F32))
        tp = ctx.enter_context(nc.psum_tensor("tp", [P, 2, KT, P], F32))
        places = [tp[:, 0, :, :], tp[:, 1, :, :], mm[:, 1, :, :].rearrange("p j (k b) -> p (j k) b", b=P)]
        transposed_to = [places[u % 3] for u in range(U_PAIR)]
        buffer_of = [0, 1, 0, 1, 2, 3, 0, 1]
        quarters = table.rearrange("r (i c) -> (r i) c", i=Q)

        def raw_buf(u):
            return u % 2

        def turned_buf(u):
            n = (u - U_PAIR) % N_TURNED
            if n >= N_TURNED - 2:
                return tp[:, n - (N_TURNED - 2), :, :]
            return nat[:, 2 + n, :].rearrange("p (k b) -> p k b", k=KT)

        def by_tile(rows):
            return rows.rearrange("p (c k) -> p k c", k=KT)

        rem_dram = nc.dram_tensor("rem_dram", [P, BT, H], F32, kind="Internal").ap()

        ids_in = sem("ids_in")
        fields_in = sem("fields_in")
        first_in = sem("first_in")
        q_ids_in = sem("q_ids_in")
        bias_in = sem("bias_in")
        dense_in = sem("dense_in")
        dense_w_in = sem("dense_w_in")
        nat_in = [sem(f"nat_in{n}") for n in range(N_NAT)]
        rem_in = [sem(f"rem_in{n}") for n in range(BT)]
        raw_in = [sem(f"raw_in{n}") for n in range(N_RAW)]
        numbered = sem("numbered")
        ident_made = sem("ident_made")
        setup_step = sem("setup_step")
        rows_ready = sem("rows_ready")
        flags_ready = sem("flags_ready")
        bias_turned = sem("bias_turned")
        bias_ready = sem("bias_ready")
        rem_used = sem("rem_used")
        rem_stored = sem("rem_stored")
        rem_back = sem("rem_back")
        rem_turned = sem("rem_turned")
        rem_mixed = sem("rem_mixed")
        tail_zeroed = sem("tail_zeroed")
        tail_turned = sem("tail_turned")
        tail_hi = sem("tail_hi")
        tail_ready = sem("tail_ready")
        w_hi_ready = sem("w_hi_ready")
        w_ready = sem("w_ready")
        w_used = sem("w_used")
        transposed = sem("transposed")
        turned = sem("turned")
        fill_hi = sem("fill_hi")
        filled = sem("filled")
        pair_hi = sem("pair_hi")
        pair_lo = sem("pair_lo")
        act_step = sem("act_step")
        evac_act = sem("evac_act")
        and_hi = sem("and_hi")
        and_ready = sem("and_ready")
        mix_step = sem("mix_step")
        not_mixed = sem("not_mixed")
        mix_sum = sem("mix_sum")
        evacuated = sem("evacuated")
        y_done = sem("y_done")
        y_ready = sem("y_ready")
        stored = sem("stored")

        block = ctx.enter_context(nc.Block())

        @block.sync
        def _(sp):
            def granule(w, k_tile, m, g, q):
                if not (isinstance(g, int) and g < N_RAW):
                    sp.wait_ge(w_ready, g - N_RAW + 1)
                src = w[k_tile * P:(k_tile + KG) * P, bass.ds(m * P, P)].rearrange("(k p) n -> p k n", p=P)
                sp.dma_start(w_raw[:, q, :, :], src).then_inc(raw_in[q], 16)

            def two_steps(parts, g0, i):
                for n in range(2 * len(parts)):
                    half, part = divmod(n, len(parts))
                    w, k_tile = parts[part]
                    granule(w, k_tile, i * 2 + half, i * (2 * len(parts)) + (g0 + n), (g0 + n) % N_RAW)

            sp.dma_start(ids_i, ids.rearrange("(t p) f -> p t f", p=P)).then_inc(ids_in, 16)
            not1 = [(Wn1, 0), (Wn1, KG)]
            two_steps(not1, G_NOT1, 0)
            with sp.Fori(1, KT // 2) as i:
                two_steps(not1, G_NOT1, i)
            with sp.Fori(0, KT // 2) as i:
                two_steps([(Wn2, 0), (Wn2, KG)], G_NOT2, i)
            def by_halves(m, g0):
                for n in range(8):
                    granule(Wa1, (n // 4 * 2 + n % 2) * KG, m + n // 2 % 2, g0 + n, (g0 + n) % N_RAW)

            by_halves(0, G_AND1)
            with sp.Fori(1, KT // 2 - 1) as i:
                two_steps([(Wa1, n * KG) for n in range(4)], G_AND1, i)
            by_halves(KT - 2, G_OR1 - 8)
            with sp.Fori(0, KT // 2) as i:
                two_steps([(Wo1, n * KG) for n in range(4)], G_OR1, i)
            with sp.Fori(0, KT // 2) as i:
                two_steps([(Wa2, 0), (Wa2, KG), (Wo2, 0), (Wo2, KG)], G_MIX, i)
            with sp.Fori(0, M1 // 2) as i:
                two_steps([(Wt1, 0), (Wt1, KG)], G_TOP1, i)
            for m in range(M2):
                granule(Wt2, 0, m, G_TOP2 + m, (G_TOP2 + m) % N_RAW)
            sp.wait_ge(y_ready, 1)
            sp.dma_start(out.rearrange("b o -> o b"), y_row).then_inc(stored, 16)
            sp.wait_ge(stored, 16)

        @block.gpsimd
        def _(pool):
            pool.iota(field_no_i, pattern=[[1, NF]], base=0, channel_multiplier=0).then_inc(numbered, 1)
            pool.memset(ident[:, :], 0.0).then_inc(ident_made, 1)
            pool.wait_ge(ident_made, 1)
            pool.affine_select(out=ident[:, :], in_=ident[:, :], compare_op=ALU.not_equal, fill=1.0, base=0,
                               pattern=[[-1, P]], channel_multiplier=1).then_inc(ident_made, 1)


            def gather(rows, tab, index, signal):
                pool.indirect_dma_start(rows, None, tab,
                                        bass.IndirectOffsetOnAxis(ap=index, axis=0)).then_inc(signal, 16)

            def gather_quarters(u):
                slot, bt = divmod(u, BT)
                if u < U_PAIR + 2:
                    pool.wait_ge(transposed, U_PAIR)
                else:
                    pool.wait_ge(turned, u - U_PAIR - 1)
                for g in range(Q):
                    n = bt * Q + g
                    gather(nat[:, raw_buf(u), g * (H // Q):(g + 1) * (H // Q)], quarters,
                           quarter_rows[:, n, slot - 2:slot - 1], nat_in[raw_buf(u)])

            pool.wait_ge(rows_ready, 1)
            for u in range(U_PAIR):
                slot, bt = divmod(u, BT)
                if u >= N_NAT:
                    pool.wait_ge(transposed, u - N_NAT + 1)
                gather(nat[:, u % N_NAT, :], table, rows_i[:, bt, slot:slot + 1], nat_in[u % N_NAT])
            pool.wait_ge(rows_ready, 2)
            for f in range(NF):
                for bt in range(BT):
                    if f:
                        pool.wait_ge(rem_used, (f - 1) * BT + bt + 1)
                    gather(rem_rows[:, bt, :], table, field_rows_i[:, bt, f:f + 1], rem_in[bt])
                if f == 0:
                    pool.wait_ge(rows_ready, 3)
                    gather_quarters(U_PAIR)
                    gather_quarters(U_PAIR + 1)
            for u in range(U_PAIR + 2, U_REM):
                gather_quarters(u)
                bt = u - (U_PAIR + 5)
                if 0 <= bt < BT:
                    pool.wait_ge(rem_used, (NF - 1) * BT + bt + 1)
                    pool.dma_start(rem_dram[:, bt, :], rem_sum[:, bt, :]).then_inc(rem_stored, 16)
            pool.wait_ge(filled, U_REM)
            pool.wait_ge(rem_stored, 16 * BT)
            for i in range(Q):
                pool.dma_start(
                    nat[i * R:(i + 1) * R, 0:BT, :].rearrange("r t (g c) -> r t g c", g=Q),
                    rem_dram[:, :, i * (H // Q):(i + 1) * (H // Q)].rearrange("(g r) t c -> r t g c", g=Q),
                ).then_inc(rem_back, 16)
            pool.memset(nat[:, BT:BT + 2, 0:B], 0.0).then_inc(tail_zeroed, 1)
            pool.wait_ge(tail_zeroed, 1)
            for at in range(0, 3 * R, R):
                pool.dma_start(dense_nat[:, :, at:at + ND], dense.rearrange("(t p) d -> p t d", p=P)).then_inc(dense_in, 16)
                pool.dma_start(dense_w[at:at + ND, :], Wt1[H:H + ND, :]).then_inc(dense_w_in, 16)

        @block.tensor
        def _(pe):
            def transpose_not(u):
                pe.wait_ge(nat_in[u % N_NAT], 16 * (u // N_NAT + 1))
                if u >= len(places):
                    pe.wait_ge(filled, u - len(places) + 1)
                for k in range(KT):
                    last = pe.transpose(transposed_to[u][:, k, :], by_tile(nat[:, u % N_NAT, :])[:, k, :], ident[:, :])
                last.then_inc(transposed, 1)

            def products(bank, wh, wl, x, k, first, last):
                for j, buf in enumerate(x):
                    pe.matmul(bank[:, j, :], wh, x_hi[:, buf, k, :], start=first, stop=False)
                    pe.matmul(bank[:, j, :], wh, x_lo[:, buf, k, :], start=False, stop=False)
                for j, buf in enumerate(x):
                    ins = pe.matmul(bank[:, j, :], wl, x_hi[:, buf, k, :], start=False, stop=last)
                return ins

            def step(t, g, parity, operands, before=None, dense_m=None):
                bank = mm[:, parity, :, :]
                pe.wait_ge(evacuated, t - 1) if not (isinstance(t, int) and t < 2) else None
                if dense_m is not None:
                    pe.wait_ge(tail_ready, 2)
                    pe.matmul(bank[:, 0, :], x_hi[:, 1, TAIL_W, dense_m * P:(dense_m + 1) * P],
                              x_hi[:, 1, TAIL_X, :], start=True, stop=False)
                n = sum(size for _, size in operands)
                tiles = [(x, k) for x, size in operands for k in range(size)]
                for at, (x, k) in enumerate(tiles):
                    if at % KG == 0:
                        pe.wait_ge(w_ready, g + at // KG + 1)
                    if before and at in before:
                        pe.wait_ge(*before[at])
                    q = at // KG % N_SPLIT
                    ins = products(bank, w_hi[:, q, at % KG, :], w_lo[:, q, at % KG, :], x, k,
                                   at == 0 and dense_m is None, at == n - 1)
                    if at % KG == KG - 1:
                        ins.then_inc(w_used, 1)

            def stage(t0, g0, operands, first, last, before=None):
                granules = sum(size for _, size in operands) // KG
                with pe.Fori(first, last) as i:
                    for half in range(2):
                        step(i * 2 + (t0 + half), i * (2 * granules) + (g0 + half * granules), half, operands, before)

            pe.wait_ge(ident_made, 2)
            for _ in range(WARM_UP):
                pe.transpose(tp[:, 0, 0, :], ident[:, :], ident[:, :])
            pe.wait_ge(bias_in, 16)
            pe.transpose(mm[:, 1, 0, 0:N_BIAS], bias_raw[0:N_BIAS, :], ident[0:N_BIAS, 0:N_BIAS]).then_inc(bias_turned, 1)
            for _ in range(WARM_UP):
                pe.transpose(tp[:, 0, 0, :], ident[:, :], ident[:, :])

            transpose_not(0)
            transpose_not(1)
            pe.wait_ge(bias_ready, 1)
            transpose_not(2)
            transpose_not(3)
            amid = {(0, 0, 3): 4, (0, 0, 7): 5, (0, 1, 1): 6, (0, 1, 5): 7}
            for x in range(2):
                for half in range(2):
                    cols = slice(half * (B // 2), (half + 1) * (B // 2))
                    pe.wait_ge(filled, x * BT + (half + 1) * (BT // 2))
                    for k in range(KT):
                        q, kk = divmod(k, KG)
                        pe.wait_ge(w_ready, q + 1)
                        for n, (w, xs) in enumerate(((w_hi, x_hi), (w_hi, x_lo), (w_lo, x_hi))):
                            ins = pe.matmul(mm[:, 0, x, cols], w[:, q, kk, :], xs[:, x, k, cols],
                                            start=k == 0 and n == 0, stop=k == KT - 1 and n == 2)
                        if x == 1 and half == 1 and kk == KG - 1:
                            ins.then_inc(w_used, 1)
                        if (x, half, k) in amid:
                            transpose_not(amid[x, half, k])
            nots = [((0, 1), KT)]
            step(1, G_NOT1 + 2, 1, nots)
            stage(S_NOT1, G_NOT1, nots, 1, KT // 2)
            stage(S_NOT2, G_NOT2, [((2, 3), KT)], 0, KT // 2, {KT - 1: (evacuated, S_NOT2)})

            def by_halves(t0, g0):
                for n in range(4):
                    half, parity = divmod(n, 2)
                    if half == 0:
                        pe.wait_ge(evacuated, t0 + parity - 1)
                    elif parity == 0:
                        pe.wait_ge(filled, U_OR)
                    for k in range(KT):
                        g, kk = g0 + 2 * n + k // KG, k % KG
                        pe.wait_ge(w_ready, g + 1) if kk == 0 else None
                        if n == 0 and t0 == S_AND1:
                            pe.wait_ge(pair_lo, 2 * k + 2)
                        ins = products(mm[:, parity, :, :], w_hi[:, g % N_SPLIT, kk, :], w_lo[:, g % N_SPLIT, kk, :],
                                       (2 * half, 2 * half + 1), k, half == 0 and k == 0, half == 1 and k == KT - 1)
                        if kk == KG - 1:
                            ins.then_inc(w_used, 1)

            by_halves(S_AND1, G_AND1)
            stage(S_AND1, G_AND1, [((0, 1), KT), ((2, 3), KT)], 1, KT // 2 - 1)
            by_halves(S_OR1 - 2, G_OR1 - 8)

            stage(S_OR1, G_OR1, [((0,), KT), ((1,), KT)], 0, KT // 2,
                  {0: (filled, U_OR + BT), KT: (filled, U_REM)})

            mixed = [((2,), KT), ((3,), KT)]
            before = {KT - 1: (and_ready, KT), 2 * KT - 1: (evacuated, S_MIX)}
            step(S_MIX, G_MIX, 0, mixed, before)
            pe.wait_ge(dense_in, 3 * 16)
            pe.wait_ge(rem_mixed, BT)
            for bt in range(BT):
                last = pe.transpose(tp[:, 0, bt, :], dense_nat[:, bt, :], ident[:, :])
            last.then_inc(tail_turned, 1)
            step(S_MIX + 1, G_MIX + 4, 1, mixed, before)
            stage(S_MIX, G_MIX, mixed, 1, KT // 2, before)

            for m in range(M1):
                step(S_TOP1 + m, G_TOP1 + 2 * m, m % 2, [((0,), KT)], {KT - 1: (evacuated, S_TOP1)}, dense_m=m)
            pe.wait_ge(evacuated, S_TOP2 - 1)
            for tiles in (range(KG - 1), range(KG - 1, KG)):
                for m in range(M2):
                    pe.wait_ge(w_ready, G_TOP2 + m + 1)
                    if tiles[0]:
                        pe.wait_ge(evacuated, S_TOP2)
                    for k in tiles:
                        q = (G_TOP2 + m) % N_SPLIT
                        ins = products(mm[:, 0, m:m + 1, :], w_hi[:, q, k, :], w_lo[:, q, k, :], (1,), k, k == 0,
                                       k == KG - 1)
                    if tiles[0]:
                        ins.then_inc(w_used, 1)
            for m in range(M2):
                pe.wait_ge(evac_act, S_TOP2 + m + 1)
                last = pe.matmul(mm[0:1, 1, 0, :], bias[:, C_W3 + m:C_W3 + m + 1], top_out[:, m, :],
                                 start=m == 0, stop=m == M2 - 1)
            last.then_inc(y_done, 1)

        def column(c, m):
            return bias[:, bass.ds(m + c, 1)]

        def tile(t, m):
            return t[:, bass.ds(m, 1), :].rearrange("p k b -> p (k b)")

        def load_flags(engine, slots, is_not_field, which_not):
            engine.wait_ge(flags_ready, 1)
            for s in slots:
                is_not_field[s] = engine.value_load(flags[0:1, 0, s:s + 1], min_val=0, max_val=1)
                which_not[s] = engine.value_load(flags[0:1, 1, s:s + 1], min_val=0, max_val=1)

        @block.scalar
        def _(act):
            act.dma_start(fields_i, fields.partition_broadcast(P)).then_inc(fields_in, 16)
            act.dma_start(first_i, first_row.partition_broadcast(P)).then_inc(first_in, 16)
            act.dma_start(bias_raw[0:N_BIAS, :], bias_rows).then_inc(bias_in, 16)
            for i in range(Q):
                act.dma_start(q_ids_i[i * R:(i + 1) * R, :, :],
                              ids.rearrange("(t r) f -> r t f", r=R)).then_inc(q_ids_in, 16)

            def split(c, i=0, per=0):
                g = i * per + c
                act.wait_ge(raw_in[c % N_RAW], i * (16 * (per // N_RAW)) + 16 * (c // N_RAW + 1))
                if c >= N_SPLIT:
                    act.wait_ge(w_used, g - N_SPLIT + 1)
                act.activation(w_hi[:, c % N_SPLIT, :, :], w_raw[:, c % N_RAW, :, :], ACT.Copy).then_inc(w_hi_ready, 1)

            idle = iter(range(idle_act.shape[1]))

            def nothing(signal):
                n = next(idle)
                act.activation(idle_act[:, n:n + 1], ident[:, 0:1], ACT.Copy).then_inc(signal, 1)

            def fills(u0, n):
                for u in range(u0, u0 + n):
                    fill(u)

            def fill(u):
                slot, bt = divmod(u, BT)
                to = x_hi[:, buffer_of[slot], :, bt * P:(bt + 1) * P]
                if slot < 2:
                    act.wait_ge(transposed, u + 1)
                    act.activation(to, transposed_to[u], ACT.Copy).then_inc(fill_hi, 1)
                    return
                act.wait_ge(turned, u - U_PAIR + 1)
                if slot < 4:
                    with act.If(is_not_field[slot] == 0):
                        act.activation(to, turned_buf(u), ACT.Copy).then_inc(fill_hi, 1)
                    with act.Else():
                        nothing(fill_hi)
                    return
                with act.If(is_not_field[slot] == 0):
                    act.activation(to, turned_buf(u), ACT.Copy).then_inc(fill_hi, 1)
                with act.Else():
                    of = tanh_out[:, bass.ds(which_not[slot], 1), :, bt * P:(bt + 1) * P]
                    act.activation(to, of.rearrange("p a k b -> p (a k) b"), ACT.Copy).then_inc(fill_hi, 1)

            def to_hidden(bufs, c):
                def evac(m, t, parity):
                    n = len(bufs)
                    for j in range(n):
                        act.activation(mm[:, parity, j, :], mm[:, parity, j, :], ACT.Relu,
                                       bias=column(c, m)).then_inc(act_step, 1)
                    act.wait_ge(act_step, act_base[c] + m * n + n)
                    for j, buf in enumerate(bufs):
                        last = act.activation(tile(x_hi[:, buf, :, :], m), mm[:, parity, j, :], ACT.Copy)
                    last.then_inc(evac_act, 1)
                return evac

            act_base = {C_N1: 0, C_O1: 2 * KT, C_T1: 3 * KT}

            def not2_evac(m, t, parity):
                act.wait_ge(rem_used, NF * BT)
                for j in range(2):
                    last = act.activation(tile(tanh_out[:, j, :, :], m), mm[:, parity, j, :], ACT.Tanh,
                                          bias=column(C_N2, m))
                last.then_inc(evac_act, 1)
                act.wait_ge(evac_act, t + 1)
                for buf in range(2):
                    with act.If(is_not_field[2 + buf] == 1):
                        of = tanh_out[:, bass.ds(which_not[2 + buf], 1), m, :]
                        act.activation(x_hi[:, buf, m, :], of.rearrange("p a b -> p (a b)"), ACT.Copy).then_inc(pair_hi, 1)
                    with act.Else():
                        nothing(pair_hi)

            def and_evac(m, t, parity):
                act.activation(tile(and_hidden, m), mm[:, parity, 0, :], ACT.Relu, bias=column(C_A1, m))
                act.activation(mm[:, parity, 1, :], mm[:, parity, 1, :], ACT.Relu,
                               bias=column(C_A1, m)).then_inc(evac_act, 1)

            def or_evac(m, t, parity):
                act.activation(tile(x_hi[:, 2, :, :], m), tile(and_hidden, m), ACT.Copy).then_inc(and_hi, 1)
                to_hidden((3,), C_O1)(m, t, parity)

            def mix_evac(m, t, parity):
                act.wait_ge(mix_sum, m + 1)
                act.activation(tile(x_hi[:, 0, :, :], m), tile(tanh_out[:, 0, :, :], m), ACT.Copy,
                               scale=one_by_count[:, 0:1]).then_inc(evac_act, 1)

            def step(i, half, t0, g0, granules, evac):
                per = 2 * granules
                c = g0 + half * granules
                for n in range(2, granules + 2):
                    split(c + n, i, per)
                act.wait_ge(w_used, i * per + c + granules)
                evac(i * 2 + half, i * 2 + (t0 + half), half)

            def stage(t0, g0, granules, evac, first=0, last=KT // 2):
                with act.Fori(first, last) as i:
                    for half in range(2):
                        step(i, half, t0, g0, granules, evac)

            split(0)
            split(1)
            fills(0, U_PAIR)
            act.wait_ge(bias_ready, 1)
            step(0, 0, S_NOT1, G_NOT1, 2, to_hidden((2, 3), C_N1))
            step(0, 1, S_NOT1, G_NOT1, 2, to_hidden((2, 3), C_N1))
            stage(S_NOT1, G_NOT1, 2, to_hidden((2, 3), C_N1), 1, 3)
            is_not_field, which_not = {}, {}
            load_flags(act, range(2, N_SLOTS), is_not_field, which_not)
            stage(S_NOT1, G_NOT1, 2, to_hidden((2, 3), C_N1), 3)
            for m in range(KT):
                c = G_NOT2 + 2 * m
                split(c + 2)
                split(c + 3)
                act.wait_ge(w_used, c + 2)
                not2_evac(m, S_NOT2 + m, m % 2)
                if m < BT:
                    fills(U_PAIR + 2 * m, 2)
            fills(U_SECOND, 2)
            split(G_AND1 + 2)
            fills(U_SECOND + 2, 2)
            split(G_AND1 + 3)
            fills(U_SECOND + 4, 4)
            for n in range(4, 7):
                split(G_AND1 + n)
            act.wait_ge(w_used, G_AND1 + 6)
            act.wait_ge(rem_stored, 16 * BT)
            and_evac(0, S_AND1, 0)
            for n in range(7, 10):
                split(G_AND1 + n)
            act.wait_ge(w_used, G_AND1 + 8)
            and_evac(1, S_AND1 + 1, 1)
            stage(S_AND1, G_AND1, 4, and_evac, 1, KT // 2 - 1)
            for n in range(-6, -3):
                split(G_OR1 + n)
            act.wait_ge(w_used, G_OR1 - 4)
            fills(U_OR, 2)
            split(G_OR1 - 3)
            fills(U_OR + 2, 2)
            split(G_OR1 - 2)
            fills(U_OR + 4, 2)
            split(G_OR1 - 1)
            act.wait_ge(w_used, G_OR1 - 2)
            and_evac(KT - 2, S_OR1 - 2, 0)
            fills(U_OR + 6, 2)
            split(G_OR1)
            split(G_OR1 + 1)
            act.wait_ge(w_used, G_OR1)
            and_evac(KT - 1, S_OR1 - 1, 1)
            stage(S_OR1, G_OR1, 4, or_evac)

            step(0, 0, S_MIX, G_MIX, 4, mix_evac)
            act.wait_ge(tail_turned, 1)
            act.activation(x_hi[:, 1, TAIL_X, :], tp[:, 0, 0:BT, :].rearrange("p t b -> p (t b)"),
                           ACT.Copy).then_inc(tail_hi, 1)
            act.wait_ge(dense_w_in, 3 * 16)
            act.activation(x_hi[:, 1, TAIL_W, :], dense_w, ACT.Copy).then_inc(tail_hi, 1)
            step(0, 1, S_MIX, G_MIX, 4, mix_evac)
            stage(S_MIX, G_MIX, 4, mix_evac, 1)

            for m in range(M1):
                c = G_TOP1 + 2 * m
                split(c + 2)
                split(c + 3)
                act.wait_ge(w_used, c + 2)
                to_hidden((1,), C_T1)(m, S_TOP1 + m, m % 2)
            for m in range(M2):
                act.wait_ge(w_used, G_TOP2 + m + 1)
                act.activation(top_out[:, m, :], mm[:, 0, m, :], ACT.Relu, bias=column(C_T2, m)).then_inc(evac_act, 1)
            act.wait_ge(y_done, 1)
            act.activation(y_row, mm[0:1, 1, 0, :], ACT.Copy).then_inc(y_ready, 1)

        @block.vector
        def _(dve):
            done = [0]

            def link(ins):
                done[0] += 1
                ins.then_inc(setup_step, 1)
                dve.wait_ge(setup_step, done[0])

            dve.wait_ge(fields_in, 16)
            dve.wait_ge(numbered, 1)
            dve.tensor_copy(fields_f, fields_i).then_inc(setup_step, 1)
            dve.tensor_copy(field_no, field_no_i).then_inc(setup_step, 1)
            dve.wait_ge(ids_in, 16)
            dve.wait_ge(first_in, 16)
            dve.tensor_copy(ids_f, ids_i).then_inc(setup_step, 1)
            done[0] = 3
            link(dve.tensor_copy(first_f, first_i))
            dve.tensor_tensor(ids_f, ids_f, first_f.unsqueeze(1).to_broadcast([P, BT, NF]), ALU.add).then_inc(setup_step, 1)
            done[0] = 5
            link(dve.tensor_tensor(is_field, fields_f.unsqueeze(2).to_broadcast([P, N_SLOTS, NF]),
                                   field_no.unsqueeze(1).to_broadcast([P, N_SLOTS, NF]), ALU.is_equal))
            link(dve.tensor_tensor(picked, is_field[:, 0:2, :].unsqueeze(1).to_broadcast([P, BT, 2, NF]),
                                   ids_f.unsqueeze(2).to_broadcast([P, BT, 2, NF]), ALU.mult))
            link(dve.tensor_reduce(rows_f, picked, AX.X, ALU.add))
            dve.tensor_copy(rows_i[:, :, :], rows_f).then_inc(rows_ready, 1)
            dve.tensor_copy(field_rows_i[:, :, :], ids_f).then_inc(rows_ready, 1)

            def split(c, i=0, per=0):
                dve.wait_ge(w_hi_ready, i * per + c + 1)
                dve.tensor_tensor(w_lo[:, c % N_SPLIT, :, :], w_raw[:, c % N_RAW, :, :],
                                  w_hi[:, c % N_SPLIT, :, :].bitcast(F32), ALU.subtract).then_inc(w_ready, 1)

            def turn(u):
                n = u - U_PAIR
                dve.wait_ge(nat_in[raw_buf(u)], 16 * X_USES[raw_buf(u)] + 16 * Q * (n // 2 + 1))
                if n >= N_TURNED:
                    dve.wait_ge(filled, u - N_TURNED + 1)
                dve.transpose(turned_buf(u).rearrange("p k (g r) -> p g k r", g=Q),
                              nat[:, raw_buf(u), :].rearrange("p (g c k) -> p g k c", g=Q, k=KT)).then_inc(turned, 1)

            idle = iter(range(idle_dve.shape[1]))

            def nothing(signal):
                n = next(idle)
                dve.memset(idle_dve[:, n:n + 1], 0.0).then_inc(signal, 1)

            def fills(u0, n):
                for u in range(u0, u0 + n):
                    fill(u)

            def fill(u):
                slot, bt = divmod(u, BT)
                buf, cols = buffer_of[slot], slice(bt * P, (bt + 1) * P)
                to, hi = x_lo[:, buf, :, cols], x_hi[:, buf, :, cols].bitcast(F32)
                dve.wait_ge(fill_hi, u + 1)
                if slot < 2:
                    dve.tensor_tensor(to, transposed_to[u], hi, ALU.subtract).then_inc(filled, 1)
                    return
                if slot < 4:
                    with dve.If(is_not_field[slot] == 0):
                        dve.tensor_tensor(to, turned_buf(u), hi, ALU.subtract).then_inc(filled, 1)
                    with dve.Else():
                        nothing(filled)
                    return
                with dve.If(is_not_field[slot] == 0):
                    dve.tensor_tensor(to, turned_buf(u), hi, ALU.subtract).then_inc(filled, 1)
                with dve.Else():
                    of = tanh_out[:, bass.ds(which_not[slot], 1), :, cols].rearrange("p a k b -> p (a k) b")
                    dve.tensor_tensor(to, of, hi, ALU.subtract).then_inc(filled, 1)

            def lo_part(buf, m, src):
                return dve.tensor_tensor(tile(x_lo[:, buf, :, :], m), src,
                                         tile(x_hi[:, buf, :, :], m).bitcast(F32), ALU.subtract)

            def to_hidden(bufs):
                def evac(m, t, parity):
                    dve.wait_ge(evac_act, t + 1)
                    for j, buf in enumerate(bufs):
                        last = lo_part(buf, m, mm[:, parity, j, :])
                    last.then_inc(evacuated, 1)
                return evac

            def not2_evac(m, t, parity):
                dve.wait_ge(evac_act, t + 1)
                dve.sem_inc(evacuated, 1)
                for buf in range(2):
                    dve.wait_ge(pair_hi, 2 * m + buf + 1)
                    with dve.If(is_not_field[2 + buf] == 1):
                        of = tanh_out[:, bass.ds(which_not[2 + buf], 1), m, :]
                        dve.tensor_tensor(x_lo[:, buf, m, :], of.rearrange("p a b -> p (a b)"),
                                          x_hi[:, buf, m, :].bitcast(F32), ALU.subtract).then_inc(pair_lo, 1)
                    with dve.Else():
                        nothing(pair_lo)

            def and_evac(m, t, parity):
                dve.wait_ge(evac_act, t + 1)
                dve.tensor_tensor(tile(and_hidden, m), tile(and_hidden, m), mm[:, parity, 1, :],
                                  ALU.add).then_inc(evacuated, 1)

            def or_evac(m, t, parity):
                dve.wait_ge(and_hi, m + 1)
                lo_part(2, m, tile(and_hidden, m)).then_inc(and_ready, 1)
                to_hidden((3,))(m, t, parity)

            def weight_nots(m):
                t0, t1 = (tanh_out[:, j, bass.ds(m * 2, 2), :].rearrange("p k b -> p (k b)") for j in range(2))
                dve.tensor_scalar(t0, t0, rem_t[:, 0:1], None, ALU.mult).then_inc(mix_step, 1)
                dve.wait_ge(mix_step, m + 1)
                dve.scalar_tensor_tensor(t0, t1, rem_t[:, 1:2], t0, ALU.mult, ALU.add).then_inc(not_mixed, 1)

            def turn_rem(bt):
                dve.wait_ge(rem_back, 16 * Q)
                dve.transpose(tp[:, bt % 2, :, :].rearrange("p k (g r) -> p g k r", g=Q),
                              nat[:, bt, :].rearrange("p (g c k) -> p g k c", g=Q, k=KT)).then_inc(rem_turned, 1)

            def add_rem(bt):
                dve.wait_ge(not_mixed, KT // 2)
                dve.wait_ge(rem_turned, bt + 1)
                part = tanh_out[:, 0, :, bt * P:(bt + 1) * P]
                dve.tensor_tensor(part, part, tp[:, bt % 2, :, :], ALU.add).then_inc(rem_mixed, 1)

            def mix_evac(m, t, parity):
                z = tile(tanh_out[:, 0, :, :], m)
                dve.wait_ge(w_used, mix_used(m))
                dve.scalar_tensor_tensor(z, mm[:, parity, 0, :], mix_bias[:, bass.ds(m, 1)], z, ALU.add,
                                         ALU.add).then_inc(mix_sum, 1)
                dve.wait_ge(evac_act, t + 1)
                dve.scalar_tensor_tensor(tile(x_lo[:, 0, :, :], m), z, one_by_count[:, 0:1],
                                         tile(x_hi[:, 0, :, :], m).bitcast(F32), ALU.mult,
                                         ALU.subtract).then_inc(evacuated, 1)

            def mix_used(m):
                return m * 4 + (G_MIX + 4)

            def step(i, half, t0, g0, granules, evac, amid={}):
                per = 2 * granules
                c = g0 + half * granules
                m = i * 2 + half
                for n in range(2, granules + 2):
                    split(c + n, i, per)
                    if n in amid:
                        amid[n](m)
                evac(m, i * 2 + (t0 + half), half)

            def stage(t0, g0, granules, evac, first=0, last=KT // 2):
                with dve.Fori(first, last) as i:
                    for half in range(2):
                        step(i, half, t0, g0, granules, evac)

            def not1_evac(m, t, parity):
                to_hidden((2, 3))(m, t, parity)
                add_field(m)

            def add_field(m):
                if not isinstance(m, int) or m:
                    dve.wait_ge(rem_used, m * BT)
                for bt in range(BT):
                    dve.wait_ge(rem_in[bt], m * 16 + 16)
                    if isinstance(m, int) and m == 0:
                        dve.tensor_scalar(rem_sum[:, bt, :], rem_rows[:, bt, :], rem_e[:, 0:1], None,
                                          ALU.mult).then_inc(rem_used, 1)
                        continue
                    dve.scalar_tensor_tensor(rem_sum[:, bt, :], rem_rows[:, bt, :], rem_e[:, bass.ds(m, 1)],
                                             rem_sum[:, bt, :], ALU.mult, ALU.add).then_inc(rem_used, 1)

            def which_remain():
                link(dve.tensor_reduce(paired, is_field[:, 2:N_SLOTS, :].rearrange("p s f -> p f s"), AX.X, ALU.max))
                link(dve.tensor_scalar(remains, paired, -1.0, 1.0, ALU.mult, ALU.add))
                link(dve.tensor_reduce(other[:, 0:1], remains, AX.X, ALU.add))
                link(dve.tensor_scalar(other[:, 0:1], other[:, 0:1], float((N_SLOTS - 2) // 2), None, ALU.add))
                dve.reciprocal(one_by_count[:, :], other[:, 0:1]).then_inc(setup_step, 1)
                done[0] += 1
                link(dve.tensor_tensor(no_not, is_field[:, 0, :], is_field[:, 1, :], ALU.max))
                link(dve.tensor_scalar(no_not, no_not, -1.0, 1.0, ALU.mult, ALU.add))
                link(dve.tensor_tensor(rem_e[:, :], remains, no_not, ALU.mult))
            def which_fields():
                for a in range(2):
                    last = dve.tensor_tensor(pair_of[:, a, :, :], is_field,
                                             is_field[:, a, :].unsqueeze(1).to_broadcast([P, N_SLOTS, NF]), ALU.mult)
                link(last)
                link(dve.tensor_reduce(is_not[:, 0:2, :], pair_of, AX.X, ALU.add))
                dve.tensor_tensor(flags[:, 0, :], is_not[:, 0, :], is_not[:, 1, :], ALU.max).then_inc(setup_step, 1)
                done[0] += 1
                link(dve.tensor_scalar(flags[:, 1, :], is_not[:, 0, :], -1.0, 1.0, ALU.mult, ALU.add))
                link(dve.tensor_tensor(pair_of[:, 0, 0:2, :], is_field[:, 0:2, :],
                                       remains.unsqueeze(1).to_broadcast([P, 2, NF]), ALU.mult))
                link(dve.tensor_reduce(rem_t[:, :], pair_of[:, 0, 0:2, :], AX.X, ALU.add))
                link(dve.tensor_scalar(other[:, 1:2], is_not[:, 0, 1:2], -1.0, 1.0, ALU.mult, ALU.add))
                link(dve.tensor_tensor(rem_t[:, 1:2], rem_t[:, 1:2], other[:, 1:2], ALU.mult))
                dve.sem_inc(flags_ready, 1)

            dve.wait_ge(bias_turned, 1)
            link(dve.tensor_copy(bias[:, :], mm[:, 1, 0, 0:N_BIAS]))
            dve.scalar_tensor_tensor(mix_bias[:, :], bias[:, C_A2:C_A2 + KT], 2.0, bias[:, C_O2:C_O2 + KT],
                                     ALU.mult, ALU.add).then_inc(bias_ready, 1)

            split(0)
            split(1)
            fills(0, U_PAIR)

            NS = N_SLOTS - 2
            dve.wait_ge(q_ids_in, 16 * Q)
            for i in range(Q):
                dve.memset(quadrant[i * R:(i + 1) * R, :], float(i)).then_inc(setup_step, 1)
            done[0] += Q
            link(dve.tensor_copy(q_ids_f, q_ids_i))
            link(dve.tensor_tensor(q_ids_f, q_ids_f, first_f.unsqueeze(1).to_broadcast([P, BT * Q, NF]), ALU.add))
            link(dve.tensor_tensor(q_picked, is_field[:, 2:N_SLOTS, :].unsqueeze(1).to_broadcast([P, BT * Q, NS, NF]),
                                   q_ids_f.unsqueeze(2).to_broadcast([P, BT * Q, NS, NF]), ALU.mult))
            link(dve.tensor_reduce(q_rows_f, q_picked, AX.X, ALU.add))
            dve.tensor_scalar(quarter_rows[:, :, :], q_rows_f, float(Q), quadrant[:, 0:1], ALU.mult,
                              ALU.add).then_inc(rows_ready, 1)

            for c in range(2, 4):
                split(c)
            to_hidden((2, 3))(0, S_NOT1, 0)
            which_remain()
            add_field(0)
            step(0, 1, S_NOT1, G_NOT1, 2, not1_evac, {2: lambda _: which_fields()})
            stage(S_NOT1, G_NOT1, 2, not1_evac, 1, 3)
            is_not_field, which_not = {}, {}
            load_flags(dve, (2, 3), is_not_field, which_not)
            stage(S_NOT1, G_NOT1, 2, not1_evac, 3)
            turned_at = [range(U_PAIR + 2 * m, U_PAIR + 2 * m + 2) for m in range(6)]
            turned_at += [(U_PAIR + 12,), (U_PAIR + 13,)]
            for m in range(KT):
                split(G_NOT2 + 2 * m + 2)
                split(G_NOT2 + 2 * m + 3)
                not2_evac(m, S_NOT2 + m, m % 2)
                if m == 5:
                    load_flags(dve, (4, 5), is_not_field, which_not)
                for u in turned_at[m]:
                    turn(u)
                if m < BT:
                    fills(U_PAIR + 2 * m, 2)
            fills(U_SECOND, 2)
            split(G_AND1 + 2)
            turn(U_SECOND + 6)
            fills(U_SECOND + 2, 2)
            split(G_AND1 + 3)
            turn(U_SECOND + 7)
            fills(U_SECOND + 4, 4)
            for n in range(4, 7):
                split(G_AND1 + n)
            and_evac(0, S_AND1, 0)
            for n in range(7, 10):
                split(G_AND1 + n)
            and_evac(1, S_AND1 + 1, 1)
            turn(U_OR)
            for m in range(2, KT - 2):
                step(m // 2, m % 2, S_AND1, G_AND1, 4, and_evac)
                if m == 2:
                    load_flags(dve, (6, 7), is_not_field, which_not)
                turn(U_OR - 1 + m)
            for n in range(-6, -3):
                split(G_OR1 + n)
            turn(U_OR + 5)
            fills(U_OR, 2)
            split(G_OR1 - 3)
            turn(U_OR + 6)
            fills(U_OR + 2, 2)
            split(G_OR1 - 2)
            turn(U_OR + 7)
            fills(U_OR + 4, 2)
            split(G_OR1 - 1)
            and_evac(KT - 2, S_OR1 - 2, 0)
            fills(U_OR + 6, 2)
            split(G_OR1)
            split(G_OR1 + 1)
            and_evac(KT - 1, S_OR1 - 1, 1)
            dve.wait_ge(evacuated, S_OR1)
            with dve.Fori(0, KT // 4) as i:
                for half in range(2):
                    step(i, half, S_OR1, G_OR1, 4, or_evac, {2: weight_nots})
            for m in range(KT // 2, KT):
                step(m // 2, m % 2, S_OR1, G_OR1, 4, or_evac,
                     {2: lambda m: turn_rem(m - KT // 2), 4: lambda m: add_rem(m - KT // 2)})
            dve.wait_ge(rem_mixed, BT)
            step(0, 0, S_MIX, G_MIX, 4, mix_evac)
            dve.wait_ge(tail_hi, 1)
            dve.tensor_tensor(x_hi[LO_X, 1, TAIL_X, :], tp[LO_X, 0, 0:BT, :].rearrange("p t b -> p (t b)"),
                              x_hi[LO_X, 1, TAIL_X, :].bitcast(F32), ALU.subtract).then_inc(tail_ready, 1)
            dve.wait_ge(tail_hi, 2)
            dve.tensor_tensor(x_hi[LO_W, 1, TAIL_W, :], dense_w[LO_W, :], x_hi[LO_W, 1, TAIL_W, :].bitcast(F32),
                              ALU.subtract).then_inc(tail_ready, 1)
            step(0, 1, S_MIX, G_MIX, 4, mix_evac)
            stage(S_MIX, G_MIX, 4, mix_evac, 1)
            for m in range(M1):
                c = G_TOP1 + 2 * m
                split(c + 2) if c + 2 < G_TOP2 + M2 else None
                split(c + 3) if c + 3 < G_TOP2 + M2 else None
                to_hidden((1,))(m, S_TOP1 + m, m % 2)


def kernel(dense_ctx, ids, tbl_0, tbl_1, tbl_2, tbl_3, tbl_4, tbl_5, tbl_6, tbl_7, W_top1, b_top1, W_top2, b_top2,
           W_top3, L0_rec_Wn1, L0_rec_bn1, L0_rec_Wn2, L0_rec_bn2, L0_rec_Wa1, L0_rec_ba1, L0_rec_Wa2, L0_rec_ba2,
           L0_rec_Wo1, L0_rec_bo1, L0_rec_Wo2, L0_rec_bo2, L0_rec_not_idx, L0_rec_and_pairs, L0_rec_or_pairs):
    import numpy as np
    import concourse.bacc as bacc
    from concourse.bass_utils import run_bass_kernel_spmd

    tables = [tbl_0, tbl_1, tbl_2, tbl_3, tbl_4, tbl_5, tbl_6, tbl_7]
    sizes = [t.shape[0] for t in tables]
    H_TILES = tbl_0.shape[1] // P
    arrays = {
        "dense": dense_ctx,
        "ids": ids,
        "fields": np.concatenate([np.ravel(L0_rec_not_idx), np.ravel(np.transpose(L0_rec_and_pairs)),
                                  np.ravel(L0_rec_or_pairs)]),
        "table": np.concatenate(tables).reshape(-1, H_TILES, P).transpose(0, 2, 1).reshape(-1, H_TILES * P),
        "first_row": np.array([sum(sizes[:n]) for n in range(len(sizes))], np.int32),
        "Wn1": L0_rec_Wn1, "Wn2": L0_rec_Wn2, "Wa1": L0_rec_Wa1, "Wa2": L0_rec_Wa2,
        "Wo1": L0_rec_Wo1, "Wo2": L0_rec_Wo2, "Wt1": W_top1, "Wt2": W_top2,
        "bias_rows": np.concatenate([L0_rec_bn1, L0_rec_bn2, L0_rec_ba1, L0_rec_ba2, L0_rec_bo1, L0_rec_bo2,
                                     b_top1, b_top2, np.ravel(W_top3)]).reshape(-1, P),
    }
    arrays = {k: np.ascontiguousarray(v) for k, v in arrays.items()}
    nc = bacc.Bacc("TRN2", target_bir_lowering=False, num_devices=1, dynamic_dma_scratch_size=SCRATCH)
    aps = {k: nc.dram_tensor(k, v.shape, mybir.dt.from_np(v.dtype), kind="ExternalInput").ap()
           for k, v in arrays.items()}
    out = nc.dram_tensor("out", (ids.shape[0], 1), F32, kind="ExternalOutput").ap()
    logic_tower(nc, *aps.values(), out)
    return run_bass_kernel_spmd(nc, [arrays], core_ids=[0]).results[0]["out"]
```
